# Optimizing a Trainium2 kernel written in Bass

```python
import numpy as np
import jax
import jax.numpy as jnp

def _softmax(x, axis=-1):
    return jax.nn.softmax(x, axis=axis)

def _gelu(x):
    return jax.nn.gelu(x, approximate=True)

def _silu(x):
    return jax.nn.silu(x)

def _sigmoid(x):
    return jax.nn.sigmoid(x)

def _layernorm(x, axis=-1, eps=1e-05):
    m = jnp.mean(x, axis=axis, keepdims=True)
    v = jnp.var(x, axis=axis, keepdims=True)
    return (x - m) / jnp.sqrt(v + eps)

def _scatter_add(tgt, idx, src, axis=0):
    return tgt.at[idx].add(src)

def _segment_sum(src, seg, n):
    return jax.ops.segment_sum(src, seg, n)
kernel_name = 'mk_adj_ffn_d1_adj_r2_4bbfe2'

def setup_inputs(seed: int=0):
    np.random.seed(seed)
    _w = jnp.asarray

    def _rec_inputs():
        import jax
        import jax.numpy as jnp
        _gk = jax.random.key(seed)
        x = -0.0002928 + 1 * jax.random.normal(jax.random.fold_in(_gk, 1), (16, 512, 128), jnp.float32)
        _w = (1.0 + jnp.arange(512, dtype=jnp.float32)) ** (-0.5)
        _w = _w / _w.mean()
        _pij = jnp.clip(0.015625 * _w[:, None] * _w[None, :], 0.0, 1.0)
        _a = jax.random.uniform(jax.random.fold_in(_gk, 2), (16, 512, 512)) < _pij
        _a = jnp.logical_or(_a, jnp.swapaxes(_a, -1, -2))
        _a = jnp.logical_or(_a, jnp.eye(512, dtype=bool))
        _af = _a.astype(jnp.float32)
        _af = _af * jax.random.uniform(jax.random.fold_in(_gk, 3), (16, 512, 512), jnp.float32, 0.05, 1)
        adj = _af
        return (x, adj)
    x, adj = _rec_inputs()

    def _L0_gnn_setup():
        import jax, jax.numpy as jnp
        import numpy as np
        LN_EPS = 1e-05
        key = jax.random.key(seed)
        k1, k2, k3, k4 = jax.random.split(key, 4)
        B, N, F, O = (8, 1024, 128, 128)
        x = jax.random.normal(k1, (B, N, F), dtype=jnp.float32)
        adj = jax.random.uniform(k2, (B, N, N), dtype=jnp.float32)
        gamma = jnp.ones((F,), jnp.float32)
        beta = jnp.zeros((F,), jnp.float32)
        W_self = jax.random.normal(k3, (F, O), dtype=jnp.float32) * (1.0 / np.sqrt(F))
        W_neigh = jax.random.normal(k4, (F, O), dtype=jnp.float32) * (1.0 / np.sqrt(F))
        return {'x': x, 'adj': adj, 'gamma': gamma, 'beta': beta, 'W_self': W_self, 'W_neigh': W_neigh}
    _L0_gnn_all = _L0_gnn_setup()
    _L0_gnn_in = {k: v for k, v in _L0_gnn_all.items() if k in ('gamma', 'beta', 'W_self', 'W_neigh')}
    del _L0_gnn_all

    def _L0_ffn_setup():
        import jax, jax.numpy as jnp
        import numpy as np
        D_MODEL = 128
        EXPERT_DIM = 256
        NUM_EXPERTS = 8
        TOP_K = 2
        SEQ_LEN = 1024
        BATCH = 2
        key = jax.random.key(seed)
        ks = jax.random.split(key, 8)
        s = 0.02
        x = jax.random.normal(ks[0], (SEQ_LEN, BATCH, D_MODEL), dtype=jnp.float32)
        Wg = jax.random.normal(ks[1], (D_MODEL, NUM_EXPERTS), dtype=jnp.float32) * s
        bg = jax.random.normal(ks[2], (NUM_EXPERTS,), dtype=jnp.float32) * s
        bias = jnp.zeros((NUM_EXPERTS,), dtype=jnp.float32)
        W1 = jax.random.normal(ks[3], (NUM_EXPERTS, D_MODEL, EXPERT_DIM), dtype=jnp.float32) * s
        b1 = jax.random.normal(ks[4], (NUM_EXPERTS, EXPERT_DIM), dtype=jnp.float32) * s
        W2 = jax.random.normal(ks[5], (NUM_EXPERTS, EXPERT_DIM, D_MODEL), dtype=jnp.float32) * s
        b2 = jax.random.normal(ks[6], (NUM_EXPERTS, D_MODEL), dtype=jnp.float32) * s
        return {'x': x, 'Wg': Wg, 'bg': bg, 'bias': bias, 'W1': W1, 'b1': b1, 'W2': W2, 'b2': b2}
    _L0_ffn_all = _L0_ffn_setup()
    _L0_ffn_in = {k: v for k, v in _L0_ffn_all.items() if k in ('Wg', 'bg', 'bias', 'W1', 'b1', 'W2', 'b2')}
    del _L0_ffn_all
    return {'x': x, 'adj': adj, 'L0_gnn_gamma': _L0_gnn_in['gamma'], 'L0_gnn_beta': _L0_gnn_in['beta'], 'L0_gnn_W_self': _L0_gnn_in['W_self'], 'L0_gnn_W_neigh': _L0_gnn_in['W_neigh'], 'L0_ffn_Wg': _L0_ffn_in['Wg'], 'L0_ffn_bg': _L0_ffn_in['bg'], 'L0_ffn_bias': _L0_ffn_in['bias'], 'L0_ffn_W1': _L0_ffn_in['W1'], 'L0_ffn_b1': _L0_ffn_in['b1'], 'L0_ffn_W2': _L0_ffn_in['W2'], 'L0_ffn_b2': _L0_ffn_in['b2']}

def reference(x, adj, L0_gnn_gamma, L0_gnn_beta, L0_gnn_W_self, L0_gnn_W_neigh, L0_ffn_Wg, L0_ffn_bg, L0_ffn_bias, L0_ffn_W1, L0_ffn_b1, L0_ffn_W2, L0_ffn_b2):
    import jax
    import jax.numpy as jnp

    def _L0_gnn_ref(x, adj, gamma, beta, W_self, W_neigh):
        import jax, jax.numpy as jnp
        import numpy as np
        LN_EPS = 1e-05
        mu = jnp.mean(x, axis=-1, keepdims=True)
        var = jnp.mean(jnp.square(x - mu), axis=-1, keepdims=True)
        xn = (x - mu) * jax.lax.rsqrt(var + LN_EPS) * gamma + beta
        d_out = jnp.sum(adj, axis=1)
        d_in = jnp.sum(adj, axis=2)
        s_out = jnp.where(d_out != 0, jax.lax.rsqrt(d_out), 0.0)
        s_in = jnp.where(d_in != 0, jax.lax.rsqrt(d_in), 0.0)
        A_norm = s_out[:, :, None] * adj * s_in[:, None, :]
        eye = jnp.eye(adj.shape[1], dtype=adj.dtype)
        L = eye[None, :, :] - A_norm
        neighbor = jnp.einsum('bij,bjf->bif', L, xn)
        pre = xn @ W_self + neighbor @ W_neigh
        return jax.nn.softplus(pre)

    def _L0_ffn_ref(x, Wg, bg, bias, W1, b1, W2, b2):
        import jax, jax.numpy as jnp
        import numpy as np
        D_MODEL = 128
        EXPERT_DIM = 256
        NUM_EXPERTS = 8
        TOP_K = 2
        SEQ_LEN = 1024
        BATCH = 2
        x_flat = x.reshape(-1, D_MODEL)
        gate_logits = x_flat @ Wg + bg + bias
        topk_vals, topk_idx = jax.lax.top_k(gate_logits, TOP_K)
        topk_w = jax.nn.softmax(topk_vals, axis=-1)
        combine = (jax.nn.one_hot(topk_idx, NUM_EXPERTS, dtype=x.dtype) * topk_w[..., None]).sum(axis=1)
        h = jax.nn.relu(jnp.einsum('td,edh->teh', x_flat, W1) + b1)
        y = jnp.einsum('teh,ehd->ted', h, W2) + b2
        out = jnp.einsum('ted,te->td', y, combine)
        return out.reshape(x.shape)
    x = x + _L0_gnn_ref(_layernorm(x, axis=-1), adj, L0_gnn_gamma, L0_gnn_beta, L0_gnn_W_self, L0_gnn_W_neigh)
    x = x + _L0_ffn_ref(_layernorm(x, axis=-1), L0_ffn_Wg, L0_ffn_bg, L0_ffn_bias, L0_ffn_W1, L0_ffn_b1, L0_ffn_W2, L0_ffn_b2)
    return x

_drawn_inputs = setup_inputs


def setup_inputs(seed=0):
    import zlib

    import numpy as np

    out = dict(_drawn_inputs(seed))
    spreads = {'L0_gnn_gamma': (1.0, 0.2), 'L0_gnn_beta': (0.0, 0.1), 'L0_ffn_bias': (0.0, 0.426)}
    factors = {'L0_ffn_bg': 8.0, 'L0_ffn_W1': 2.902, 'L0_ffn_b1': 28.597, 'L0_ffn_b2': 5.932}
    for name, (base, spread) in spreads.items():
        noise = np.random.default_rng([zlib.crc32(name.encode()), seed]).standard_normal(out[name].shape)
        drawn = base * np.exp(spread * noise) if base else spread * noise
        out[name] = jnp.asarray(drawn.astype(out[name].dtype))
    for name, factor in factors.items():
        out[name] = (out[name] * factor).astype(out[name].dtype)
    return out
```

```python
from contextlib import ExitStack

import concourse.bass as bass
from concourse import mybir

F32 = mybir.dt.float32
BF16 = mybir.dt.bfloat16
F16 = mybir.dt.float16
I32 = mybir.dt.int32
ALU = mybir.AluOpType
ACT = mybir.ActivationFunctionType
AX_X = mybir.AxisListType.X
RMAX = bass.bass_isa.ReduceOp.max

P = 128
EPS = 1e-5


def gnn_moe_kernel(nc, x, adj, gamma, beta, w_self, w_neigh, w_gate, b_gate, bias_gate, w1, b1, w2, b2, out):
    B, N, D = x.shape
    E, _, H = w1.shape
    T = N // P
    HC = H // P
    TOKENS = B * N
    PAIRS = [(a, b) for a in range(E) for b in range(a + 1, E)]
    NPAIR = len(PAIRS)
    REGION = TOKENS + P
    DUMMY = NPAIR * REGION
    FULL = TOKENS // P
    TILES = FULL + NPAIR
    ROW = D + 8
    MEAN, RSTD, WA, TOKEN = D, D + 1, D + 2, D + 4
    SKIPPED = 1 << 20
    TURNS = B // 2
    assert N == T * P == 512 and D == P and E == 8 and B % 2 == 0 and HC == 2

    sorted_rows = nc.dram_tensor("sorted_rows", (DUMMY + P, ROW), F32, kind="Internal").ap()
    x_v = x.rearrange("b (t p) d -> b p t d", p=P)
    adj_v = adj.rearrange("b (t p) j -> b p t j", p=P)
    out_rows = out.rearrange("b n d -> (b n) d")

    with ExitStack() as ctx:
        def sb(name, shape, dt=F32):
            return ctx.enter_context(nc.sbuf_tensor(name, shape, dt))

        def pair_of(name, shape, dt=F32):
            return [sb(f"{name}{i}", shape, dt) for i in range(2)]

        def bank(name):
            return ctx.enter_context(nc.psum_tensor(name, [P, 512], F32))

        def sem(name):
            return ctx.enter_context(nc.semaphore(name))

        def sem2(name):
            return [sem(f"{name}{i}") for i in range(2)]

        ident = sb("ident", [P, P])
        ones_bf = sb("ones_bf", [P, P], BF16)
        before = sb("before", [P, P], BF16)
        upto = sb("upto", [P, P], BF16)
        one_row = sb("one_row", [1, P])
        zero4 = sb("zero4", [P, T], I32)
        zero_i = sb("zero_i", [P, 1], I32)
        zero_bf = sb("zero_bf", [P, P], BF16)
        p_row = sb("p_row", [1, P])
        step4 = sb("step4", [P, T], I32)
        gamma_b = sb("gamma_b", [P, D])
        beta_b = sb("beta_b", [P, D])
        w_self_s = sb("w_self_s", [P, D])
        w_neigh_s = sb("w_neigh_s", [P, D])
        w_sum = sb("w_sum", [P, D])
        w_gate_s = sb("w_gate_s", [P, E])
        gate_row = sb("gate_row", [1, 2, E])
        gate_bias = sb("gate_bias", [1, T, E])
        rev = sb("rev", [P, E])
        codes = sb("codes", [P, NPAIR])
        pair_base = sb("pair_base", [1, T, NPAIR])
        pair_base_all = sb("pair_base_all", [P, NPAIR])
        pair_a = sb("pair_a", [P, NPAIR])
        pair_b = sb("pair_b", [P, NPAIR])
        tile_no = sb("tile_no", [P, 1])
        w1f = sb("w1f", [P, E, H])
        w2f = sb("w2f", [P, E, HC, D])
        w1h = sb("w1h", [P, E * H], F16)
        w1l = sb("w1l", [P, E * H], F16)
        w2h = sb("w2h", [P, E * HC * D], F16)
        w2l = sb("w2l", [P, E * HC * D], F16)
        b1p = sb("b1p", [P, E * H], BF16)
        b2p = sb("b2p", [P, E * D], BF16)
        NB1, NB2 = E * H // P, E * D // P
        bv = sb("bv", [P, NB1 + NB2])
        brest = sb("brest", [P, 2, NB1 + NB2])
        bpart = sb("bpart", [P, 3, NB1 + NB2], BF16)
        peak = sb("peak", [P, 4])
        peak2 = sb("peak2", [P, 2])
        peak_all = sb("peak_all", [P, 2])
        peak_c = sb("peak_c", [P, 2])
        expo = sb("expo", [P, 2], I32)
        scale_f = sb("scale_f", [P, 2])
        inv_f = sb("inv_f", [P, 2])
        scale12 = sb("scale12", [P, 1])
        inv12 = sb("inv12", [P, 1])
        blank_rows = sb("blank_rows", [P, ROW])

        adj_s = pair_of("adj_s", [P, T, N])
        adj_t = pair_of("adj_t", [P, T, N])
        junk = sb("junk", [P, T, N], BF16)
        x_s = pair_of("x_s", [P, T, D])
        xr_s = pair_of("xr_s", [P, T, D])
        st = pair_of("st", [P, T, 6])
        mv = pair_of("mv", [P, T, 2])
        rs = pair_of("rs", [P, 4, T])
        rstd = pair_of("rstd", [P, T])
        u_s = pair_of("u_s", [P, T, D])
        xn_s = pair_of("xn_s", [P, T, D])
        xn_t = pair_of("xn_t", [P, T * P])
        deg = pair_of("deg", [P, 2, T])
        deg_c = pair_of("deg_c", [P, 2, T])
        deg_w = pair_of("deg_w", [P, 4, 2, T])
        s_deg = pair_of("s_deg", [P, 2, T])
        s_neg = pair_of("s_neg", [P, T])
        sxn = pair_of("sxn", [P, T, D])
        z_t = pair_of("z_t", [P, T * P])
        p_s = pair_of("p_s", [P, T * D])
        pre = pair_of("pre", [P, T * D])
        pre_c = pair_of("pre_c", [P, T * D])
        sp = pair_of("sp", [P, T, D])
        pay = pair_of("pay", [P, T, ROW])
        st2 = pair_of("st2", [P, T, 6])
        mv2 = pair_of("mv2", [P, T, 2])
        rs2 = pair_of("rs2", [P, 4, T])
        x2 = pair_of("x2", [P, T, D])
        x2_t = pair_of("x2_t", [P, T * P])
        lo8 = pair_of("lo8", [P, T, E])
        eq8 = pair_of("eq8", [P, T, E])
        ky8 = pair_of("ky8", [P, T, E])
        l28 = pair_of("l28", [P, T, E])
        m4 = pair_of("m4", [P, 6, T])
        e4 = pair_of("e4", [P, T])
        w4 = pair_of("w4", [P, 6, T])
        pick = pair_of("pick", [P, T, NPAIR], BF16)
        picked = pair_of("picked", [P, T, NPAIR])
        slot_f = pair_of("slot_f", [P, T])
        slot = pair_of("slot", [P, T], I32)
        tid = pair_of("tid", [P, T], I32)

        base_all = sb("base_all", [P, NPAIR])
        rest_no = sb("rest_no", [P, 1])
        any_pair = sb("any_pair", [P, 1])
        tab_cols = sb("tab_cols", [P, 3])
        cnt_i = sb("cnt_i", [P, 2, NPAIR], I32)
        n_full = sb("n_full", [P, NPAIR])
        ends = sb("ends", [P, NPAIR])
        starts = sb("starts", [P, NPAIR])
        inside = sb("inside", [P, 4, NPAIR])
        row_of = sb("row_of", [P, NPAIR])
        vals = sb("vals", [P, 5])
        tile_row = sb("tile_row", [P, 4])
        prod = sb("prod", [P, 5, NPAIR])
        ones_pair = sb("ones_pair", [P, NPAIR])
        rest_of = sb("rest_of", [P, NPAIR])
        rest_row = sb("rest_row", [P, NPAIR])
        table = sb("table", [1, 3, P], I32)
        pad_row = sb("pad_row", [1, NPAIR], I32)

        rows_in = sb("rows_in", [P, TILES, ROW])
        token = pair_of("token", [P, 1], I32)
        tn = pair_of("tn", [P, D])
        th = pair_of("th", [P, P], F16)
        tl = pair_of("tl", [P, P], F16)
        hh = pair_of("hh", [P, 2 * HC * P], F16)
        hl = pair_of("hl", [P, 2 * HC * P], F16)
        ya = pair_of("ya", [P, D])
        yb = pair_of("yb", [P, D])
        yo = pair_of("yo", [P, D])

        bank_a = [bank("bank_a0"), bank("bank_a1")]
        bank_x = bank("bank_x")
        bank_z = bank("bank_z")
        bank_p = bank("bank_p")
        bank_g = bank("bank_g")
        bank_l = bank("bank_l")
        bank_r = bank("bank_r")
        logits_p = bank_l[:, 0:T * E]
        rank_p = bank_r[:, 0:T * NPAIR]
        bank_t, bank_h, bank_y = [bank_x, bank_z], bank_a, [bank_p, bank_g]

        consts_in, weights_in = sem("consts_in"), sem("weights_in")
        adj_in, x_in, xr_in = sem2("adj_in"), sem2("x_in"), sem2("xr_in")
        scattered = sem2("scattered")
        bias_placed = sem("bias_placed")
        pads_out = sem("pads_out")
        tile_loaded = [sem(f"tile_loaded{i}") for i in range(2)]
        stored = sem2("stored")
        pool_c, dve_c, act_c, peak_ready = sem("pool_c"), sem("dve_c"), sem("act_c"), sem("peak_ready")
        var_ready, y_ready = sem("var_ready"), sem("y_ready")
        u_ready, ug_ready, xn_ready = sem("u_ready"), sem("ug_ready"), sem("xn_ready")
        xn_t_made, xn_t_ready = sem("xn_t_made"), sem("xn_t_ready")
        adj_t_made, adj_t_ready = sem("adj_t_made"), sem("adj_t_ready")
        deg_ready, degy_ready, sxn_ready = sem("deg_ready"), sem("degy_ready"), sem("sxn_ready")
        z_made, z_ready, p_made, p_ready = sem("z_made"), sem("z_ready"), sem("p_made"), sem("p_ready")
        g_made, pre_ready, lg_ready, sp_ready = sem("g_made"), sem("pre_ready"), sem("lg_ready"), sem("sp_ready")
        x1_ready, var2_ready, y2_ready, x2_ready = sem("x1_ready"), sem("var2_ready"), sem("y2_ready"), sem("x2_ready")
        x2_t_made, x2_t_ready = sem("x2_t_made"), sem("x2_t_ready")
        logits_made, logits_read, gap_ready, e_ready = sem("logits_made"), sem("logits_read"), sem("gap_ready"), sem("e_ready")
        row_ready, pick_ready, rank_made, slot_ready = sem("row_ready"), sem("pick_ready"), sem("rank_made"), sem("slot_ready")
        pay_ready = sem("pay_ready")
        degc_ready, w_ready, counted = sem("degc_ready"), sem("w_ready"), sem("counted")
        dve1, dve2, dve3, dve4, dve5, dve6, dve7, dve8 = (sem(f"dve{i}") for i in range(1, 9))
        act1, act2, act3, act4 = (sem(f"act{i}") for i in range(1, 5))
        pool2, pool3 = sem("pool2"), sem("pool3")
        count_made, tab_steps, tab_ready, tab_t, tab_row = (
            sem("count_made"), sem("tab_steps"), sem("tab_ready"), sem("tab_t"), sem("tab_row"))
        tn_ready, t_made, th_ready, tl_ready = sem("tn_ready"), sem("t_made"), sem("th_ready"), sem("tl_ready")
        h_made, hh_ready, hl_ready = sem("h_made"), sem("hh_ready"), sem("hl_ready")
        y_made, ya_ready, yb_ready, yo_ready = sem("y_made"), sem("ya_ready"), sem("yb_ready"), sem("yo_ready")

        class graph:

            def __init__(self, n, turn, par):
                self.n, self.turn, self.par = n, turn, par

        def pipeline(eng, count, stages, step, between=None):
            def at(i):
                return graph(i, i // 2, i % 2) if 0 <= i < count else None

            peeled = 2 * ((stages + 2) // 2)
            for i in range(peeled):
                step(*[at(i - j) for j in range(stages)])
                if between:
                    between(i)
            with eng.Fori(peeled // 2, count // 2) as turn:
                for par in range(2):
                    step(*[graph(turn * 2 + (par - j), turn + (par - j) // 2, (par - j) % 2)
                           for j in range(stages)])
            for i in range(count, count + stages - 1):
                step(*[at(i - j) for j in range(stages)])

        def after(eng, signal, value):
            if not isinstance(value, int) or value > 0:
                eng.wait_ge(signal, value)

        def apart(eng, met, signal, value):
            if not isinstance(value, int):
                value = eng.to_reg(value)
            eng.wait_ge(*met)
            eng.wait_ge(signal, value)

        class Steps:

            def __init__(self, eng, own, n, per):
                self.eng, self.own, self.base, self.per, self.n = eng, own, n * per, per, 0

            def then(self, ins, met=None):
                self.n += 1
                assert self.n <= self.per
                ins.then_inc(self.own, 1)
                if met:
                    apart(self.eng, met, self.own, self.base + self.n)
                else:
                    self.eng.wait_ge(self.own, self.base + self.n)

            def close(self):
                assert self.n == self.per, (self.n, self.per)

        def each(ap, n):
            return ap.unsqueeze(2).broadcast_to([P, T, n])

        def per_tile(ap, n):
            return ap.unsqueeze(1).broadcast_to([P, T, n])

        LOADS = 11
        POOL_BLANK, POOL_ALL = 6, 20
        DVE_GATE, DVE_PEAK, DVE_BIAS, DVE_ALL = 2, 4, 4 + 12, 4 + 12 + 2
        ACT_W = 2

        block = ctx.enter_context(nc.Block())

        @block.sync
        def _(sp_e):
            def load_graph(g):
                after(sp_e, adj_t_made, T * (g.n - 1))
                after(sp_e, deg_ready, g.n - 1)
                sp_e.dma_start(adj_s[g.par][:], adj_v[g.n]).then_inc(adj_in[g.par], 16)
                after(sp_e, u_ready, g.n - 1)
                sp_e.dma_start(x_s[g.par][:], x_v[g.n]).then_inc(x_in[g.par], 16)
                after(sp_e, x1_ready, g.n - 1)
                sp_e.dma_start(xr_s[g.par][:], x_v[g.n]).then_inc(xr_in[g.par], 16)

            def load_rest(i):
                if i == 0:
                    for dst, src in ((gamma_b[:], gamma.partition_broadcast(P)), (beta_b[:], beta.partition_broadcast(P)),
                                     (w_self_s[:], w_self), (w_neigh_s[:], w_neigh), (w_gate_s[:], w_gate),
                                     (gate_row[:, 0, :], b_gate.unsqueeze(0)),
                                     (gate_row[:, 1, :], bias_gate.unsqueeze(0))):
                        sp_e.dma_start(dst, src).then_inc(consts_in, 16)
                if i == 1:
                    b1_v = b1.rearrange("e h -> (e h)").rearrange("(p c) -> p c", p=P)
                    b2_v = b2.rearrange("e d -> (e d)").rearrange("(p c) -> p c", p=P)
                    for dst, src in ((w1f[:], w1.rearrange("e d h -> d e h")),
                                     (w2f[:], w2.rearrange("e (c h) d -> h e c d", h=P)),
                                     (bv[:, 0:NB1], b1_v), (bv[:, NB1:NB1 + NB2], b2_v)):
                        sp_e.dma_start(dst, src).then_inc(weights_in, 16)
                    sp_e.wait_ge(pool_c, POOL_BLANK)
                    sp_e.dma_start(sorted_rows[DUMMY:DUMMY + P, :], blank_rows[:]).then_inc(pads_out, 16)

            pipeline(sp_e, B, 1, load_graph, load_rest)

            sp_e.wait_ge(pool_c, POOL_ALL)
            sp_e.wait_ge(dve_c, DVE_BIAS)
            for part in range(3):
                sp_e.dma_start(b1p[part:part + 1, :], bpart[:, part, 0:NB1]).then_inc(bias_placed, 16)
                sp_e.dma_start(b2p[part:part + 1, :], bpart[:, part, NB1:NB1 + NB2]).then_inc(bias_placed, 16)

            sp_e.wait_ge(tab_ready, 2)
            for par in range(2):
                sp_e.wait_ge(scattered[par], 16 * T * TURNS)
            sp_e.wait_ge(pads_out, 16)

            def load_tile(g):
                row = sp_e.value_load(table[0:1, 0, bass.ds(g.n, 1)], min_val=0, max_val=DUMMY)
                after(sp_e, tile_loaded[g.par], 16 * g.turn)
                sp_e.wait_ge(tab_ready, 2)
                sp_e.dma_start(rows_in[:, bass.ds(g.n, 1), :].rearrange("p a d -> p (a d)"),
                               sorted_rows[bass.ds(row, P), :]).then_inc(tile_loaded[g.par], 16)

            def pad(q):
                row = sp_e.value_load(pad_row[0:1, bass.ds(q, 1)], min_val=0, max_val=DUMMY)
                sp_e.dma_start(sorted_rows[bass.ds(row, P), :], blank_rows[:]).then_inc(pads_out, 16)

            for par in range(2):
                load_tile(graph(par, 0, par))
            with sp_e.Fori(1, FULL // 2) as turn:
                for par in range(2):
                    load_tile(graph(turn * 2 + par, turn, par))
            with sp_e.Fori(0, NPAIR) as q:
                pad(q)
            sp_e.wait_ge(pads_out, 16 * (NPAIR + 1))
            with sp_e.Fori(FULL // 2, TILES // 2) as turn:
                for par in range(2):
                    load_tile(graph(turn * 2 + par, turn, par))
            for par in range(2):
                sp_e.wait_ge(stored[par], 16 * (TILES // 2))

        @block.gpsimd
        def _(pool):
            count = [0]

            def made(ins, wait=False):
                count[0] += 1
                ins.then_inc(pool_c, 1)
                if wait:
                    pool.wait_ge(pool_c, count[0])

            made(pool.memset(ident[:], 0.0), True)
            made(pool.affine_select(out=ident[:], in_=ident[:], compare_op=ALU.not_equal, fill=1.0, base=0,
                                    pattern=[[-1, P]], channel_multiplier=1))
            made(pool.memset(one_row[:], 1.0))
            made(pool.memset(blank_rows[:], 0.0), True)
            made(pool.memset(blank_rows[:, TOKEN:TOKEN + 1].bitcast(I32), SKIPPED))
            made(pool.memset(zero4[:], 0))
            assert count[0] == POOL_BLANK

            def constants(i):
                if i != 0:
                    return
                made(pool.memset(step4[:], 2 * N))
                for par in range(2):
                    made(pool.memset(pay[par][:], 0.0))
                    made(pool.iota(tid[par][:], [[P, T]], base=par * N, channel_multiplier=1,
                                   allow_small_or_imprecise_dtypes=True))
                pool.wait_ge(pool_c, count[0])
                pool.memset(ones_pair[:], 1.0)
                pool.memset(zero_i[:], 0)
                pool.memset(zero_bf[:], 0.0)
                pool.memset(p_row[:], float(P))
                pool.memset(ones_bf[:], 1.0)
                made(pool.memset(b1p[:], 0.0))
                made(pool.memset(b2p[:], 0.0))
                made(pool.memset(before[:], 1.0))
                made(pool.memset(upto[:], 1.0), True)
                made(pool.affine_select(out=before[:], in_=before[:], compare_op=ALU.is_gt, fill=0.0, base=0,
                                        pattern=[[1, P]], channel_multiplier=-1))
                made(pool.affine_select(out=upto[:], in_=upto[:], compare_op=ALU.is_ge, fill=0.0, base=0,
                                        pattern=[[-1, P]], channel_multiplier=1))
                for e in range(E):
                    pool.memset(rev[:, e:e + 1], float(2 ** (E - 1 - e)))
                for q, (a, b) in enumerate(PAIRS):
                    pool.memset(codes[:, q:q + 1], float(2 ** (E - 1 - a) + 2 ** (E - 1 - b)))
                    pool.memset(pair_a[:, q:q + 1], float(a))
                    pool.memset(pair_b[:, q:q + 1], float(b))
                made(pool.iota(pair_base[:], [[0, T], [REGION // P, NPAIR]], base=0, channel_multiplier=0,
                               allow_small_or_imprecise_dtypes=True))
                made(pool.iota(pair_base_all[:], [[REGION // P, NPAIR]], base=0, channel_multiplier=0,
                               allow_small_or_imprecise_dtypes=True))
                made(pool.iota(tile_no[:], [[0, 1]], base=0, channel_multiplier=1,
                               allow_small_or_imprecise_dtypes=True))
                assert count[0] == POOL_ALL, count

            def affine(g):
                pool.wait_ge(u_ready, g.n + 1)
                after(pool, xn_t_made, g.n - 1)
                after(pool, sxn_ready, g.n - 1)
                pool.tensor_tensor(xn_s[g.par][:], u_s[g.par][:], per_tile(gamma_b[:], D),
                                   ALU.mult).then_inc(ug_ready, 1)
                pool.wait_ge(ug_ready, g.n + 1)
                pool.tensor_tensor(xn_s[g.par][:], xn_s[g.par][:], per_tile(beta_b[:], D),
                                   ALU.add).then_inc(xn_ready, 1)

            def residual(g):
                pool.wait_ge(sp_ready, g.n + 1)
                pool.wait_ge(xr_in[g.par], 16 * (g.turn + 1))
                after(pool, scattered[g.par], 16 * T * g.turn)
                pool.tensor_tensor(pay[g.par][:, :, 0:D], sp[g.par][:], xr_s[g.par][:], ALU.add).then_inc(x1_ready, 1)
                s = Steps(pool, pool2, g.n, 2)
                s.then(pool.tensor_tensor(pay[g.par][:, :, TOKEN].bitcast(I32), tid[g.par][:], zero4[:], ALU.add))
                s.then(pool.tensor_tensor(tid[g.par][:], tid[g.par][:], step4[:], ALU.add))
                s.close()

            def weights(g):
                w = w4[g.par]
                s = Steps(pool, pool3, g.n, 4)
                pool.wait_ge(w_ready, g.n + 1)
                s.then(pool.tensor_tensor(w[:, 2, :], w[:, 1, :], e4[g.par][:], ALU.mult))
                s.then(pool.tensor_tensor(w[:, 3, :], w[:, 1, :], w[:, 2, :], ALU.subtract))
                s.then(pool.tensor_tensor(w[:, 5, :], w[:, 3, :], w[:, 4, :], ALU.mult))
                s.then(pool.tensor_tensor(pay[g.par][:, :, WA], w[:, 2, :], w[:, 5, :], ALU.add))
                pool.tensor_tensor(pay[g.par][:, :, WA + 1], w[:, 1, :], w[:, 5, :],
                                   ALU.subtract).then_inc(pay_ready, 1)
                s.close()

            def scatter(g):
                n = g.n + 1 if isinstance(g.n, int) else pool.to_reg(g.n + 1)
                pool.wait_ge(pool_c, POOL_ALL)
                pool.wait_ge(pay_ready, n)
                pool.wait_ge(slot_ready, n)
                for t in range(T):
                    pool.indirect_dma_start(
                        sorted_rows[:, :], bass.IndirectOffsetOnAxis(ap=slot[g.par][:, t:t + 1], axis=0),
                        pay[g.par][:, t, :], None).then_inc(scattered[g.par], 16)

            def graphs(g1, g2, g3):
                if g1:
                    affine(g1)
                if g2:
                    residual(g2)
                if g3:
                    weights(g3)
                    scatter(g3)

            def between(i):
                constants(i)
                if i == 1:
                    pool.wait_ge(dve_c, DVE_PEAK)
                    pool.partition_all_reduce(peak_all[:], peak2[:], P, RMAX).then_inc(peak_ready, 1)

            pool.wait_ge(consts_in, 16 * 7)
            pipeline(pool, B, 3, graphs, between)

            def finish(g):
                pool.wait_ge(yb_ready, g.n + 1)
                after(pool, stored[g.par], 16 * g.turn)
                pool.wait_ge(pool_c, POOL_ALL)
                row = rows_in[:, bass.ds(g.n, 1), :].rearrange("p a d -> p (a d)")
                pool.tensor_tensor(yo[g.par][:], yb[g.par][:], row[:, 0:D], ALU.add)
                pool.tensor_tensor(token[g.par][:], row[:, TOKEN:TOKEN + 1].bitcast(I32), zero_i[:],
                                   ALU.add).then_inc(yo_ready, 1)
                apart(pool, (pool_c, POOL_ALL), yo_ready, g.n + 1)
                pool.indirect_dma_start(
                    out_rows, bass.IndirectOffsetOnAxis(ap=token[g.par][:], axis=0),
                    yo[g.par][:], None, bounds_check=TOKENS - 1, oob_is_err=False).then_inc(stored[g.par], 16)

            pipeline(pool, TILES, 4, lambda g1, g2, g3, g4: g4 and finish(g4))

        @block.scalar
        def _(act):
            act.preload_act_table_set("natural_log_exp_and_others")

            def root(dst, src, n):
                act.activation(dst[1], src, ACT.Ln).then_inc(n[0], 1)
                act.wait_ge(n[0], n[1])
                return act.activation(dst[0], dst[1], ACT.Exp, scale=-0.5)

            def first_guess(g):
                act.wait_ge(var_ready, g.n + 1)
                r = rs[g.par]
                root((r[:, 1, :], r[:, 2, :]), r[:, 0, :], (act1, g.n + 1)).then_inc(y_ready, 1)

            def sum_rows(g):
                act.wait_ge(adj_in[g.par], 16 * (g.turn + 1))
                after(act, sxn_ready, g.n - 1)
                for t in range(T):
                    last = act.activation(junk[:, t, :], adj_s[g.par][:, t, :], ACT.Copy,
                                          accum_out=deg[g.par][:, 0, t:t + 1])
                last.then_inc(deg_ready, 1)

            def evacuate(g, t):
                act.wait_ge(adj_t_made, T * g.n + t + 1)
                if t == 0:
                    after(act, z_made, g.n - 1)
                act.activation(adj_t[g.par][:, t, :], bank_a[t % 2][:], ACT.Copy,
                               accum_out=deg[g.par][:, 1, t:t + 1]).then_inc(adj_t_ready, 1)

            def degree_guess(g):
                act.wait_ge(degc_ready, g.n + 1)
                d = deg_w[g.par]
                root((d[:, 0], d[:, 1]), deg_c[g.par][:], (act2, g.n + 1)).then_inc(degy_ready, 1)

            def xn_out(g):
                act.wait_ge(xn_t_made, g.n + 1)
                after(act, p_made, g.n - 1)
                act.activation(xn_t[g.par][:], bank_x[:], ACT.Copy).then_inc(xn_t_ready, 1)

            def p_out(g):
                act.wait_ge(p_made, g.n + 1)
                after(act, pre_ready, g.n - 1)
                act.activation(p_s[g.par][:], bank_p[:], ACT.Copy).then_inc(p_ready, 1)

            def softplus(g):
                act.wait_ge(pre_ready, g.n + 1)
                after(act, x1_ready, g.n - 1)
                act.activation(pre_c[g.par][:], pre_c[g.par][:], ACT.Exp).then_inc(act3, 1)
                act.wait_ge(act3, g.n + 1)
                act.activation(sp[g.par][:].rearrange("p t d -> p (t d)"), pre_c[g.par][:], ACT.Ln, bias=1.0).then_inc(lg_ready, 1)

            def second_guess(g):
                act.wait_ge(var2_ready, g.n + 1)
                r = rs2[g.par]
                root((r[:, 1, :], r[:, 2, :]), r[:, 0, :], (act4, g.n + 1)).then_inc(y2_ready, 1)

            def x2_out(g):
                act.wait_ge(x2_t_made, g.n + 1)
                act.activation(x2_t[g.par][:], bank_x[:], ACT.Copy).then_inc(x2_t_ready, 1)

            def gate_exp(g):
                act.wait_ge(gap_ready, g.n + 1)
                after(act, scattered[g.par], 16 * T * g.turn)
                act.activation(e4[g.par][:], m4[g.par][:, 4, :], ACT.Exp).then_inc(e_ready, 1)

            def graphs(g1, g2, g3):
                if g1:
                    first_guess(g1)
                if g3:
                    x2_out(g3)
                if g1:
                    evacuate(g1, 0)
                    evacuate(g1, 1)
                    sum_rows(g1)
                if g3:
                    gate_exp(g3)
                if g1:
                    evacuate(g1, 2)
                    evacuate(g1, 3)
                if g2:
                    p_out(g2)
                if g1:
                    degree_guess(g1)
                    xn_out(g1)
                if g2:
                    softplus(g2)
                    second_guess(g2)

            def between(i):
                if i == 2:
                    act.wait_ge(weights_in, 16 * 4)
                    act.wait_ge(dve_c, DVE_BIAS)
                    act.activation(w1h[:], w1f[:].rearrange("p e h -> p (e h)"), ACT.Copy,
                                   scale=scale_f[:, 0:1]).then_inc(act_c, 1)
                    act.activation(w2h[:], w2f[:].rearrange("p e c d -> p (e c d)"), ACT.Copy,
                                   scale=scale_f[:, 1:2]).then_inc(act_c, 1)

            pipeline(act, B, 3, graphs, between)

            def lead_x(g):
                act.wait_ge(t_made, g.n + 1)
                act.activation(th[g.par][:], bank_t[g.par][:, 0:P], ACT.Copy).then_inc(th_ready, 1)

            def lead_h(g):
                act.wait_ge(h_made, g.n + 1)
                after(act, y_made, g.n - 1)
                act.activation(hh[g.par][:], bank_h[g.par][:], ACT.Relu).then_inc(hh_ready, 1)

            def first_expert(g):
                act.wait_ge(y_made, g.n + 1)
                after(act, yb_ready, g.n - 1)
                act.wait_ge(dve_c, DVE_ALL)
                row = rows_in[:, bass.ds(g.n, 1), :].rearrange("p a d -> p (a d)")
                act.activation(ya[g.par][:], bank_y[g.par][:, 0:D], ACT.Copy,
                               scale=row[:, WA:WA + 1]).then_inc(ya_ready, 1)

            def tiles(g1, g2, g3, g4):
                if g2:
                    lead_x(g2)
                if g4:
                    first_expert(g4)
                if g3:
                    lead_h(g3)

            pipeline(act, TILES, 4, tiles)

        @block.vector
        def _(dve):
            count = [0]

            def made(ins, wait=True):
                count[0] += 1
                ins.then_inc(dve_c, 1)
                if wait:
                    dve.wait_ge(dve_c, count[0])

            def newton(s, r, arg, y, t1, t2, dst):
                s.then(dve.scalar_tensor_tensor(out=t1, in0=y, scalar=-0.5, in1=arg, op0=ALU.mult, op1=ALU.mult))
                s.then(dve.tensor_tensor(t2, t1, y, ALU.mult))
                s.then(dve.scalar_tensor_tensor(out=dst, in0=t2, scalar=1.5, in1=y, op0=ALU.add, op1=ALU.mult))

            def statistics(g):
                dve.wait_ge(x_in[g.par], 16 * (g.turn + 1))
                s = Steps(dve, dve1, g.n, 2)
                for t in range(T):
                    last = dve.bn_stats(st[g.par][:, t, :], x_s[g.par][:, t, :])
                s.then(last, met=(pool_c, 1))
                for t in range(T):
                    last = dve.bn_aggr(mv[g.par][:, t, :], st[g.par][:, t, :])
                s.then(last)
                s.close()
                dve.tensor_scalar(rs[g.par][:, 0, :], mv[g.par][:, :, 1], 1.0 + EPS, EPS * EPS,
                                  ALU.mult, ALU.add).then_inc(var_ready, 1)

            def normalise(g):
                dve.wait_ge(y_ready, g.n + 1)
                r = rs[g.par]
                s = Steps(dve, dve2, g.n, 3)
                newton(s, r, r[:, 0, :], r[:, 1, :], r[:, 2, :], r[:, 3, :], rstd[g.par][:])
                s.close()
                after(dve, ug_ready, g.n - 1)
                for t in range(T):
                    last = dve.tensor_scalar(u_s[g.par][:, t, :], x_s[g.par][:, t, :], mv[g.par][:, t, 0:1],
                                             rstd[g.par][:, t:t + 1], ALU.subtract, ALU.mult)
                last.then_inc(u_ready, 1)

            def degrees(g):
                dve.wait_ge(deg_ready, g.n + 1)
                dve.wait_ge(adj_t_ready, T * (g.n + 1))
                dve.tensor_scalar(deg_c[g.par][:], deg[g.par][:], 1e-18, None, ALU.max).then_inc(degc_ready, 1)

            def scale_rows(g):
                dve.wait_ge(degy_ready, g.n + 1)
                d = deg_w[g.par]
                s = Steps(dve, dve3, g.n, 5)
                newton(s, None, deg_c[g.par][:], d[:, 0], d[:, 1], d[:, 2], d[:, 3])
                s.then(dve.tensor_scalar(d[:, 1], deg[g.par][:], 0.0, None, ALU.not_equal))
                s.then(dve.tensor_tensor(s_deg[g.par][:], d[:, 3], d[:, 1], ALU.mult))
                s.close()
                dve.wait_ge(xn_ready, g.n + 1)
                after(dve, z_made, g.n - 1)
                for t in range(T):
                    last = dve.tensor_scalar(sxn[g.par][:, t, :], xn_s[g.par][:, t, :],
                                             s_deg[g.par][:, 0, t:t + 1], None, ALU.mult)
                last.then_inc(sxn_ready, 1)

            def z_out(g):
                dve.wait_ge(z_made, g.n + 1)
                after(dve, g_made, g.n - 1)
                dve.tensor_copy(z_t[g.par][:], bank_z[:]).then_inc(z_ready, 1)

            def combine(g):
                dve.wait_ge(g_made, g.n + 1)
                dve.wait_ge(p_ready, g.n + 1)
                s = Steps(dve, dve4, g.n, 2)
                s.then(dve.tensor_scalar(s_neg[g.par][:], s_deg[g.par][:, 1, :], -1.0, None, ALU.mult))
                for t in range(T):
                    c = slice(t * D, (t + 1) * D)
                    last = dve.scalar_tensor_tensor(out=pre[g.par][:, c], in0=bank_g[:, c], scalar=s_neg[g.par][:, t:t + 1],
                                                    in1=p_s[g.par][:, c], op0=ALU.mult, op1=ALU.add)
                s.then(last)
                s.close()
                after(dve, lg_ready, g.n - 1)
                dve.tensor_scalar(pre_c[g.par][:], pre[g.par][:], 40.0, None, ALU.min).then_inc(pre_ready, 1)

            def soft(g):
                dve.wait_ge(lg_ready, g.n + 1)
                soft_s = sp[g.par][:].rearrange("p t d -> p (t d)")
                dve.tensor_tensor(soft_s, soft_s, pre[g.par][:], ALU.max).then_inc(sp_ready, 1)

            def second_norm(g):
                dve.wait_ge(x1_ready, g.n + 1)
                s = Steps(dve, dve5, g.n, 2)
                for t in range(T):
                    last = dve.bn_stats(st2[g.par][:, t, :], pay[g.par][:, t, 0:D])
                s.then(last, met=(pool_c, 1))
                for t in range(T):
                    last = dve.bn_aggr(mv2[g.par][:, t, :], st2[g.par][:, t, :])
                s.then(last)
                s.close()
                dve.tensor_scalar(rs2[g.par][:, 0, :], mv2[g.par][:, :, 1], EPS, None, ALU.add).then_inc(var2_ready, 1)

            def second_normalise(g):
                r = rs2[g.par]
                dve.wait_ge(y2_ready, g.n + 1)
                s = Steps(dve, dve6, g.n, 4)
                newton(s, r, r[:, 0, :], r[:, 1, :], r[:, 2, :], r[:, 3, :], pay[g.par][:, :, RSTD])
                s.then(dve.tensor_copy(pay[g.par][:, :, MEAN], mv2[g.par][:, :, 0]))
                s.close()
                after(dve, x2_t_made, g.n - 1)
                for t in range(T):
                    last = dve.tensor_scalar(x2[g.par][:, t, :], pay[g.par][:, t, 0:D], pay[g.par][:, t, MEAN:MEAN + 1],
                                             pay[g.par][:, t, RSTD:RSTD + 1], ALU.subtract, ALU.mult)
                last.then_inc(x2_ready, 1)

            def choose(g):
                i = g.par
                lo, eq, ky, l2, m = lo8[i][:], eq8[i][:], ky8[i][:], l28[i][:], m4[i]
                dve.wait_ge(logits_made, g.n + 1)
                after(dve, scattered[i], 16 * T * g.turn)
                s = Steps(dve, dve7, g.n, 14)
                s.then(dve.tensor_copy(lo, logits_p))
                s.then(dve.tensor_reduce(m[:, 0, :], lo, AX_X, ALU.max))
                s.then(dve.tensor_tensor(eq, lo, each(m[:, 0, :], E), ALU.is_equal))
                s.then(dve.tensor_tensor(ky, eq, per_tile(rev[:], E), ALU.mult))
                s.then(dve.tensor_reduce(m[:, 1, :], ky, AX_X, ALU.max))
                s.then(dve.tensor_tensor(eq, per_tile(rev[:], E), each(m[:, 1, :], E), ALU.is_equal))
                s.then(dve.scalar_tensor_tensor(out=l2, in0=eq, scalar=-3.0e38, in1=lo, op0=ALU.mult, op1=ALU.add))
                s.then(dve.tensor_reduce(m[:, 2, :], l2, AX_X, ALU.max))
                dve.tensor_tensor(m[:, 4, :], m[:, 2, :], m[:, 0, :], ALU.subtract).then_inc(gap_ready, 1)
                s.then(dve.tensor_tensor(eq, l2, each(m[:, 2, :], E), ALU.is_equal))
                s.then(dve.tensor_tensor(ky, eq, per_tile(rev[:], E), ALU.mult))
                s.then(dve.tensor_reduce(m[:, 3, :], ky, AX_X, ALU.max))
                dve.tensor_tensor(w4[i][:, 4, :], m[:, 1, :], m[:, 3, :], ALU.is_gt)
                s.then(dve.tensor_tensor(m[:, 5, :], m[:, 1, :], m[:, 3, :], ALU.add))
                dve.wait_ge(e_ready, g.n + 1)
                s.then(dve.tensor_scalar(w4[i][:, 0, :], e4[i][:], 1.0, None, ALU.add))
                s.then(dve.reciprocal(w4[i][:, 1, :], w4[i][:, 0, :]))
                s.close()
                dve.tensor_tensor(pick[i][:], per_tile(codes[:], NPAIR), each(m[:, 5, :], NPAIR),
                                  ALU.is_equal).then_inc(pick_ready, 1)
                dve.tensor_scalar(w4[i][:, 1, :], w4[i][:, 1, :], inv12[:], None, ALU.mult).then_inc(w_ready, 1)

            def place(g):
                i = g.par
                dve.wait_ge(rank_made, g.n + 1)
                s = Steps(dve, dve8, g.n, 2)
                s.then(dve.tensor_tensor(picked[i][:], rank_p, pick[i][:], ALU.mult))
                s.then(dve.tensor_reduce(slot_f[i][:], picked[i][:], AX_X, ALU.add))
                s.close()
                dve.tensor_copy(slot[i][:], slot_f[i][:]).then_inc(slot_ready, 1)

            def graphs(g1, g2, g3):
                if g1:
                    statistics(g1)
                if g2:
                    z_out(g2)
                if g3:
                    choose(g3)
                if g1:
                    normalise(g1)
                if g2:
                    combine(g2)
                if g1:
                    degrees(g1)
                    scale_rows(g1)
                if g2:
                    soft(g2)
                if g3:
                    place(g3)
                if g2:
                    second_norm(g2)
                    second_normalise(g2)

            def between(i):
                if i == 0:
                    dve.wait_ge(weights_in, 16 * 4)
                    dve.tensor_reduce(peak[:, 1:2], bv[:, 0:NB1], AX_X, ALU.max, apply_absolute_value=True)
                    dve.tensor_reduce(peak2[:, 1:2], w2f[:].rearrange("p e c d -> p (e c d)"), AX_X, ALU.max,
                                      apply_absolute_value=True)
                    made(dve.tensor_reduce(peak[:, 0:1], w1f[:].rearrange("p e h -> p (e h)"), AX_X, ALU.max,
                                           apply_absolute_value=True))
                    made(dve.tensor_tensor(peak2[:, 0:1], peak[:, 0:1], peak[:, 1:2], ALU.max))
                    assert count[0] == DVE_PEAK
                if i == 1:
                    dve.wait_ge(peak_ready, 1)
                    made(dve.tensor_scalar(peak_c[:], peak_all[:], 1e-30, None, ALU.max))
                    made(dve.tensor_scalar(expo[:], peak_c[:].bitcast(I32), 0x7F800000, None, ALU.bitwise_and))
                    made(dve.tensor_scalar(scale_f[:].bitcast(I32), expo[:], -1.0, float(261 << 23), ALU.mult, ALU.add))
                    made(dve.tensor_scalar(inv_f[:].bitcast(I32), expo[:], float(7 << 23), None, ALU.subtract))
                    made(dve.tensor_tensor(scale12[:], scale_f[:, 0:1], scale_f[:, 1:2], ALU.mult))
                    made(dve.tensor_tensor(inv12[:], inv_f[:, 0:1], inv_f[:, 1:2], ALU.mult))
                    dve.tensor_scalar(brest[:, 0, 0:NB1], bv[:, 0:NB1], scale_f[:, 0:1], None, ALU.mult)
                    made(dve.tensor_scalar(brest[:, 0, NB1:NB1 + NB2], bv[:, NB1:NB1 + NB2], scale12[:], None, ALU.mult))
                    made(dve.tensor_copy(bpart[:, 0, :], brest[:, 0, :]))
                    made(dve.tensor_tensor(brest[:, 1, :], brest[:, 0, :], bpart[:, 0, :], ALU.subtract))
                    made(dve.tensor_copy(bpart[:, 1, :], brest[:, 1, :]))
                    made(dve.tensor_tensor(brest[:, 0, :], brest[:, 1, :], bpart[:, 1, :], ALU.subtract))
                    made(dve.tensor_copy(bpart[:, 2, :], brest[:, 0, :]))
                    assert count[0] == DVE_BIAS, count
                if i == 3:
                    dve.wait_ge(act_c, 2)
                    made(dve.scalar_tensor_tensor(out=w1l[:], in0=w1f[:].rearrange("p e h -> p (e h)"),
                                                  scalar=scale_f[:, 0:1], in1=w1h[:], op0=ALU.mult, op1=ALU.subtract), False)
                    made(dve.scalar_tensor_tensor(out=w2l[:], in0=w2f[:].rearrange("p e c d -> p (e c d)"),
                                                  scalar=scale_f[:, 1:2], in1=w2h[:],
                                                  op0=ALU.mult, op1=ALU.subtract), False)
                    assert count[0] == DVE_ALL

            dve.wait_ge(consts_in, 16 * 7)
            made(dve.tensor_tensor(w_sum[:], w_self_s[:], w_neigh_s[:], ALU.add))
            made(dve.tensor_tensor(gate_bias[:], gate_row[:, 0, :].unsqueeze(1).broadcast_to([1, T, E]),
                                   gate_row[:, 1, :].unsqueeze(1).broadcast_to([1, T, E]), ALU.add))
            assert count[0] == DVE_GATE
            pipeline(dve, B, 3, graphs, between)

            tab = [0]

            def step(ins):
                tab[0] += 1
                ins.then_inc(tab_steps, 1)
                dve.wait_ge(tab_steps, tab[0])

            dve.wait_ge(count_made, 1)
            step(dve.tensor_scalar(base_all[:], pair_base_all[:], float(P), None, ALU.mult))
            step(dve.tensor_copy(pad_row[:], rank_p[0:1, 0:NPAIR]))
            step(dve.tensor_tensor(cnt_i[:, 0, :], rank_p[:, 0:NPAIR], base_all[:], ALU.subtract))
            step(dve.tensor_scalar(cnt_i[:, 1, :], cnt_i[:, 0, :], 7, None, ALU.logical_shift_right))
            step(dve.tensor_copy(n_full[:], cnt_i[:, 1, :]))
            step(dve.tensor_tensor_scan(ends[:], ones_pair[:], n_full[:], 0.0, ALU.mult, ALU.add))
            step(dve.tensor_tensor(starts[:], ends[:], n_full[:], ALU.subtract))
            step(dve.tensor_scalar(inside[:, 0, :], starts[:], tile_no[:], None, ALU.is_le))
            step(dve.tensor_scalar(inside[:, 1, :], ends[:], tile_no[:], None, ALU.is_gt))
            step(dve.tensor_tensor(inside[:, 2, :], inside[:, 0, :], inside[:, 1, :], ALU.mult))
            step(dve.tensor_scalar(rest_no[:], tile_no[:], -float(FULL), float(REGION // P), ALU.add, ALU.mult))
            step(dve.tensor_scalar(rest_of[:], pair_base_all[:], rest_no[:], None, ALU.is_equal))
            step(dve.tensor_tensor(inside[:, 3, :], inside[:, 2, :], rest_of[:], ALU.add))
            step(dve.scalar_tensor_tensor(out=row_of[:], in0=starts[:], scalar=-float(P), in1=base_all[:],
                                          op0=ALU.mult, op1=ALU.add))
            step(dve.scalar_tensor_tensor(out=rest_row[:], in0=n_full[:], scalar=float(P), in1=base_all[:],
                                          op0=ALU.mult, op1=ALU.add))
            step(dve.tensor_tensor(prod[:, 0, :], inside[:, 2, :], row_of[:], ALU.mult))
            step(dve.tensor_tensor(prod[:, 1, :], rest_of[:], rest_row[:], ALU.mult))
            step(dve.tensor_tensor(prod[:, 2, :], inside[:, 3, :], pair_a[:], ALU.mult))
            step(dve.tensor_tensor(prod[:, 3, :], inside[:, 3, :], pair_b[:], ALU.mult))
            step(dve.tensor_copy(prod[:, 4, :], inside[:, 2, :]))
            step(dve.tensor_reduce(vals[:], prod[:], AX_X, ALU.add))
            step(dve.tensor_reduce(any_pair[:], inside[:, 3, :], AX_X, ALU.add))
            step(dve.tensor_scalar(tile_row[:, 0:1], tile_no[:], float(P), None, ALU.mult))
            step(dve.tensor_tensor(tile_row[:, 1:2], tile_row[:, 0:1], vals[:, 4:5], ALU.mult))
            step(dve.tensor_scalar(tile_row[:, 2:3], any_pair[:], -float(DUMMY), float(DUMMY), ALU.mult, ALU.add))
            step(dve.scalar_tensor_tensor(out=tile_row[:, 3:4], in0=tile_row[:, 1:2], scalar=vals[:, 0:1],
                                          in1=tile_row[:, 2:3], op0=ALU.add, op1=ALU.add))
            step(dve.tensor_tensor(vals[:, 1:2], tile_row[:, 3:4], vals[:, 1:2], ALU.add))
            dve.tensor_copy(tab_cols[:], vals[:, 1:4]).then_inc(tab_ready, 1)
            dve.wait_ge(tab_t, 1)
            dve.tensor_copy(table[:].rearrange("p c n -> p (c n)"), bank_z[0:1, 0:3 * P]).then_inc(tab_ready, 1)

            def normal_row(g):
                dve.wait_ge(tile_loaded[g.par], 16 * (g.turn + 1))
                after(dve, t_made, g.n - 1)
                row = rows_in[:, bass.ds(g.n, 1), :].rearrange("p a d -> p (a d)")
                dve.tensor_scalar(tn[g.par][:], row[:, 0:D], row[:, MEAN:MEAN + 1], row[:, RSTD:RSTD + 1],
                                  ALU.subtract, ALU.mult).then_inc(tn_ready, 1)

            def rest_x(g):
                dve.wait_ge(th_ready, g.n + 1)
                dve.tensor_tensor(tl[g.par][:], bank_t[g.par][:, 0:P], th[g.par][:], ALU.subtract).then_inc(tl_ready, 1)

            def rest_h(g):
                dve.wait_ge(hh_ready, g.n + 1)
                dve.scalar_tensor_tensor(out=hl[g.par][:], in0=bank_h[g.par][:], scalar=0.0, in1=hh[g.par][:],
                                         op0=ALU.max, op1=ALU.subtract).then_inc(hl_ready, 1)

            def both_experts(g):
                dve.wait_ge(ya_ready, g.n + 1)
                after(dve, yo_ready, g.n - 1)
                row = rows_in[:, bass.ds(g.n, 1), :].rearrange("p a d -> p (a d)")
                dve.scalar_tensor_tensor(out=yb[g.par][:], in0=bank_y[g.par][:, D:2 * D], scalar=row[:, WA + 1:WA + 2],
                                         in1=ya[g.par][:], op0=ALU.mult, op1=ALU.add).then_inc(yb_ready, 1)

            def tiles(g1, g2, g3, g4):
                if g1:
                    normal_row(g1)
                if g2:
                    rest_x(g2)
                if g4:
                    both_experts(g4)
                if g3:
                    rest_h(g3)

            pipeline(dve, TILES, 4, tiles)

        @block.tensor
        def _(pe):
            pe.wait_ge(pool_c, POOL_BLANK)
            pe.wait_ge(dve_c, DVE_GATE)

            def turn_adj(g, t):
                if t == 0:
                    pe.wait_ge(adj_in[g.par], 16 * (g.turn + 1))
                after(pe, adj_t_ready, T * g.n + t - 1)
                for r in range(T):
                    last = pe.transpose(bank_a[t % 2][:, r * P:(r + 1) * P], adj_s[g.par][:, r, t * P:(t + 1) * P], ident[:])
                last.then_inc(adj_t_made, 1)

            def turn_xn(g):
                pe.wait_ge(xn_ready, g.n + 1)
                after(pe, x2_t_ready, g.n - 1)
                for t in range(T):
                    last = pe.transpose(bank_x[:, t * P:(t + 1) * P], xn_s[g.par][:, t, :], ident[:])
                last.then_inc(xn_t_made, 1)

            def product(g, t):
                if t == 0:
                    pe.wait_ge(sxn_ready, g.n + 1)
                    pe.wait_ge(adj_t_ready, T * (g.n + 1))
                    after(pe, z_ready, g.n)
                mm = pe.matmul(bank_z[:], sxn[g.par][:, t, :], adj_t[g.par][:, t, :], start=(t == 0), stop=(t == T - 1))
                if t == T - 1:
                    mm.then_inc(z_made, 1)

            def own_part(g):
                pe.wait_ge(xn_t_ready, g.n + 1)
                after(pe, p_ready, g.n)
                for t in range(T):
                    mm = pe.matmul(bank_p[:, t * D:(t + 1) * D], xn_t[g.par][:, t * P:(t + 1) * P], w_sum[:],
                                   start=True, stop=True)
                mm.then_inc(p_made, 1)

            def neighbour_part(g):
                pe.wait_ge(z_ready, g.n + 1)
                after(pe, pre_ready, g.n)
                for t in range(T):
                    mm = pe.matmul(bank_g[:, t * D:(t + 1) * D], z_t[g.par][:, t * P:(t + 1) * P], w_neigh_s[:],
                                   start=True, stop=True)
                mm.then_inc(g_made, 1)

            def turn_x2(g):
                pe.wait_ge(x2_ready, g.n + 1)
                pe.wait_ge(xn_t_ready, min(g.n + 2, B) if isinstance(g.n, int) else g.n + 2)
                for t in range(T):
                    last = pe.transpose(bank_x[:, t * P:(t + 1) * P], x2[g.par][:, t, :], ident[:])
                last.then_inc(x2_t_made, 1)

            def gate(g):
                after(pe, gap_ready, g.n)
                pe.matmul(logits_p, one_row[:], gate_bias[:].rearrange("p t e -> p (t e)"), start=True, stop=False,
                          skip_group_check=True)
                pe.wait_ge(x2_t_ready, g.n + 1)
                for t in range(T):
                    mm = pe.matmul(bank_l[:, t * E:(t + 1) * E], x2_t[g.par][:, t * P:(t + 1) * P], w_gate_s[:],
                                   start=False, stop=(t == T - 1), skip_group_check=True)
                mm.then_inc(logits_made, 1)

            def pair_cols(lo, hi):
                return bank_r[:, lo * NPAIR:hi * NPAIR]

            def count_before(g):
                pe.wait_ge(pick_ready, g.n + 1)
                for t in range(T):
                    mm = pe.matmul(pair_cols(t, t + 1), before[:], pick[g.par][:, t, :], start=False, stop=False,
                                   skip_group_check=True)
                    if t < T - 1:
                        pe.matmul(pair_cols(t + 1, T), ones_bf[:],
                                  pick[g.par][:, t, :].unsqueeze(1).broadcast_to([P, T - 1 - t, NPAIR]),
                                  start=False, stop=False, skip_group_check=True)
                mm.then_inc(rank_made, 1)

            def count_rest(g):
                pe.wait_ge(slot_ready, g.n + 1)
                for t in range(T):
                    mm = pe.matmul(pair_cols(t, t + 1), upto[:], pick[g.par][:, t, :], start=False, stop=False,
                                   skip_group_check=True)
                    if t > 0:
                        mm = pe.matmul(pair_cols(0, t), ones_bf[:],
                                       pick[g.par][:, t, :].unsqueeze(1).broadcast_to([P, t, NPAIR]),
                                       start=False, stop=False, skip_group_check=True)
                mm.then_inc(counted, 1)

            def graphs(g1, g2, g3, g4):
                if g3:
                    turn_x2(g3)
                if g2:
                    product(g2, 0)
                if g1:
                    turn_adj(g1, 0)
                    turn_adj(g1, 1)
                if g2:
                    product(g2, 1)
                if g3:
                    gate(g3)
                if g1:
                    turn_adj(g1, 2)
                if g2:
                    product(g2, 2)
                if g1:
                    turn_adj(g1, 3)
                if g2:
                    product(g2, 3)
                    own_part(g2)
                if g4:
                    count_rest(g4)
                if g3:
                    count_before(g3)
                if g2:
                    neighbour_part(g2)
                if g1:
                    turn_xn(g1)

            def between(i):
                if i == 0:
                    pe.wait_ge(pool_c, POOL_ALL)
                    pe.matmul(rank_p, p_row[:], pair_base[:].rearrange("p t q -> p (t q)"), start=True, stop=False,
                              skip_group_check=True)

            pipeline(pe, B, 4, graphs, between)
            pe.matmul(pair_cols(0, 1), zero_bf[:], pick[0][:, 0, :], start=False, stop=True,
                      skip_group_check=True).then_inc(count_made, 1)
            pe.wait_ge(tab_ready, 1)
            for c in range(3):
                mm = pe.matmul(bank_z[0:1, c * P:(c + 1) * P], tab_cols[:, c:c + 1], ident[:], start=True, stop=True)
            mm.then_inc(tab_t, 1)

            pe.wait_ge(tab_ready, 2)
            pe.wait_ge(bias_placed, 16 * 6)
            pe.wait_ge(dve_c, DVE_ALL)

            def turn_rows(g):
                pe.wait_ge(tn_ready, g.n + 1)
                after(pe, tl_ready, g.n - 1)
                pe.transpose(bank_t[g.par][:, 0:P], tn[g.par][:], ident[:]).then_inc(t_made, 1)

            def experts(g):
                return [pe.value_load(table[0:1, c, bass.ds(g.n, 1)], min_val=0, max_val=E - 1) for c in (1, 2)]

            def first_layer(g):
                two = experts(g)
                pe.wait_ge(tl_ready, g.n + 1)
                after(pe, hl_ready, g.n - 1)
                pe.wait_ge(tab_ready, 2)
                for k, e in enumerate(two):
                    for c in range(HC):
                        o = bank_h[g.par][:, (k * HC + c) * P:(k * HC + c + 1) * P]
                        w = bass.ds(e * H + c * P, P)
                        pe.matmul(o, b1p[:, w], ones_bf[:], start=True, stop=False)
                        pe.matmul(o, w1l[:, w], th[g.par][:], start=False, stop=False)
                        pe.matmul(o, w1h[:, w], tl[g.par][:], start=False, stop=False)
                        mm = pe.matmul(o, w1h[:, w], th[g.par][:], start=False, stop=True)
                mm.then_inc(h_made, 1)

            def second_layer(g):
                two = experts(g)
                pe.wait_ge(hl_ready, g.n + 1)
                after(pe, yb_ready, g.n - 1)
                pe.wait_ge(tab_ready, 2)
                for k, e in enumerate(two):
                    o = bank_y[g.par][:, k * D:(k + 1) * D]
                    pe.matmul(o, ones_bf[:], b2p[:, bass.ds(e * D, D)], start=True, stop=False)
                    for c in range(HC):
                        w = bass.ds(e * (HC * D) + c * D, D)
                        lead, rest = (v[g.par][:, (k * HC + c) * P:(k * HC + c + 1) * P] for v in (hh, hl))
                        pe.matmul(o, rest, w2h[:, w], start=False, stop=False)
                        pe.matmul(o, lead, w2l[:, w], start=False, stop=False)
                        mm = pe.matmul(o, lead, w2h[:, w], start=False, stop=(c == HC - 1))
                mm.then_inc(y_made, 1)

            def tiles(g1, g2, g3, g4):
                if g2:
                    turn_rows(g2)
                if g3:
                    first_layer(g3)
                if g4:
                    second_layer(g4)

            pipeline(pe, TILES, 4, tiles)


_INS = ["x", "adj", "L0_gnn_gamma", "L0_gnn_beta", "L0_gnn_W_self", "L0_gnn_W_neigh", "L0_ffn_Wg", "L0_ffn_bg",
        "L0_ffn_bias", "L0_ffn_W1", "L0_ffn_b1", "L0_ffn_W2", "L0_ffn_b2"]


def kernel(**inputs):
    import numpy as _np
    import concourse.bacc as _bacc
    from concourse import mybir as _mybir
    from concourse.bass_utils import run_bass_kernel_spmd as _run

    nc = _bacc.Bacc("TRN2", target_bir_lowering=False, num_devices=1)
    arrays, args = {}, []
    for name in _INS:
        a = _np.ascontiguousarray(inputs[name])
        arrays[f"in_{name}_dram"] = a
        args.append(nc.dram_tensor(f"in_{name}_dram", a.shape, _mybir.dt.from_np(a.dtype), kind="ExternalInput").ap())
    shape = inputs["x"].shape
    args.append(nc.dram_tensor("out_dram", shape, _mybir.dt.float32, kind="ExternalOutput").ap())
    gnn_moe_kernel(nc, *args)
    r = _run(nc, [arrays], core_ids=[0])
    return r.results[0]["out_dram"]
```

```python
from contextlib import ExitStack

import concourse.bass as bass
from concourse import mybir

F32 = mybir.dt.float32
BF16 = mybir.dt.bfloat16
F16 = mybir.dt.float16
I32 = mybir.dt.int32
ALU = mybir.AluOpType
ACT = mybir.ActivationFunctionType
AX_X = mybir.AxisListType.X
RMAX = bass.bass_isa.ReduceOp.max

P = 128
EPS = 1e-5


def gnn_moe_kernel(nc, x, adj, gamma, beta, w_self, w_neigh, w_gate, b_gate, bias_gate, w1, b1, w2, b2, out):
    B, N, D = x.shape
    E, _, H = w1.shape
    T = N // P
    HC = H // P
    TOKENS = B * N
    PAIRS = [(a, b) for a in range(E) for b in range(a + 1, E)]
    NPAIR = len(PAIRS)
    REGION = TOKENS + P
    DUMMY = NPAIR * REGION
    FULL = TOKENS // P
    TILES = FULL + NPAIR
    ROW = D + 8
    MEAN, RSTD, WA, TOKEN = D, D + 1, D + 2, D + 4
    SKIPPED = 1 << 20
    TURNS = B // 2
    assert N == T * P == 512 and D == P and E == 8 and B % 2 == 0 and HC == 2

    sorted_rows = nc.dram_tensor("sorted_rows", (DUMMY + P, ROW), F32, kind="Internal").ap()
    b1_parts = nc.dram_tensor("b1_parts", (3, E * H), BF16, kind="Internal").ap()
    b2_parts = nc.dram_tensor("b2_parts", (3, E * D), BF16, kind="Internal").ap()
    x_v = x.rearrange("b (t p) d -> b p t d", p=P)
    adj_v = adj.rearrange("b (t p) j -> b p t j", p=P)
    out_rows = out.rearrange("b n d -> (b n) d")

    with ExitStack() as ctx:
        def sb(name, shape, dt=F32):
            return ctx.enter_context(nc.sbuf_tensor(name, shape, dt))

        def pair_of(name, shape, dt=F32):
            return [sb(f"{name}{i}", shape, dt) for i in range(2)]

        def bank(name):
            return ctx.enter_context(nc.psum_tensor(name, [P, 512], F32))

        def sem(name):
            return ctx.enter_context(nc.semaphore(name))

        def sem2(name):
            return [sem(f"{name}{i}") for i in range(2)]

        ident = sb("ident", [P, P])
        ones_bf = sb("ones_bf", [P, P], BF16)
        before = sb("before", [P, P], BF16)
        upto = sb("upto", [P, P], BF16)
        one_row = sb("one_row", [1, P])
        zero4 = sb("zero4", [P, T], I32)
        zero_i = sb("zero_i", [P, 1], I32)
        zero_bf = sb("zero_bf", [P, P], BF16)
        p_row = sb("p_row", [1, P])
        step4 = sb("step4", [P, T], I32)
        gamma_b = sb("gamma_b", [P, D])
        beta_b = sb("beta_b", [P, D])
        w_self_s = sb("w_self_s", [P, D])
        w_neigh_s = sb("w_neigh_s", [P, D])
        w_sum = sb("w_sum", [P, D])
        w_gate_s = sb("w_gate_s", [P, E])
        gate_row = sb("gate_row", [1, 2, E])
        gate_bias = sb("gate_bias", [1, T, E])
        rev = sb("rev", [P, E])
        codes = sb("codes", [P, NPAIR])
        pair_base = sb("pair_base", [1, T, NPAIR])
        pair_base_all = sb("pair_base_all", [P, NPAIR])
        pair_a = sb("pair_a", [P, NPAIR])
        pair_b = sb("pair_b", [P, NPAIR])
        tile_no = sb("tile_no", [P, 1])
        w1f = sb("w1f", [P, E, H])
        w2f = sb("w2f", [P, E, HC, D])
        w_all = sb("w_all", [P, E, 4, H], F16)
        NB1, NB2 = E * H // P, E * D // P
        b_all = sb("b_all", [P, E, H + D], BF16)
        bv = sb("bv", [P, NB1 + NB2])
        brest = sb("brest", [P, 2, NB1 + NB2])
        bpart = sb("bpart", [P, 3, NB1 + NB2], BF16)
        peak = sb("peak", [P, 4])
        peak2 = sb("peak2", [P, 2])
        peak_all = sb("peak_all", [P, 2])
        peak_c = sb("peak_c", [P, 2])
        expo = sb("expo", [P, 2], I32)
        scale_f = sb("scale_f", [P, 2])
        inv_f = sb("inv_f", [P, 2])
        scale12 = sb("scale12", [P, 1])
        inv12 = sb("inv12", [P, 1])
        blank_rows = sb("blank_rows", [P, ROW])

        rows_in = sb("rows_in", [P, TILES, ROW])
        shared = rows_in[:].rearrange("p a d -> p (a d)")
        used = [0]

        def view(dims):
            lo = used[0]
            used[0] += dims[0] * dims[1]
            assert used[0] <= TILES * ROW
            return shared[:, lo:used[0]].rearrange("p (a b) -> p a b", a=dims[0])

        adj_s = [view([T, N]) for _ in range(2)]
        adj_t = [view([T, N]) for _ in range(2)]
        junk = sb("junk", [P, T, N], BF16)
        x_s = [view([T, D]) for _ in range(2)]
        xr_s = [view([T, D]) for _ in range(2)]
        sxn = [view([T, D]) for _ in range(2)]
        z_t = [view([1, T * P]) for _ in range(2)]
        st = pair_of("st", [P, T, 6])
        mv = pair_of("mv", [P, T, 2])
        rs = pair_of("rs", [P, 4, T])
        rstd = pair_of("rstd", [P, T])
        u_s = pair_of("u_s", [P, T, D])
        xn_s = pair_of("xn_s", [P, T, D])
        xn_t = pair_of("xn_t", [P, T * P])
        deg = pair_of("deg", [P, 2, T])
        deg_c = pair_of("deg_c", [P, 2, T])
        deg_w = pair_of("deg_w", [P, 4, 2, T])
        s_deg = pair_of("s_deg", [P, 2, T])
        s_neg = pair_of("s_neg", [P, T])
        shift2 = pair_of("shift2", [P, T])
        p_s = pair_of("p_s", [P, T * D])
        pre = pair_of("pre", [P, T * D])
        pre_c = pair_of("pre_c", [P, T * D])
        sp = pair_of("sp", [P, T, D])
        pay = pair_of("pay", [P, T, ROW])
        st2 = pair_of("st2", [P, T, 6])
        mv2 = pair_of("mv2", [P, T, 2])
        rs2 = pair_of("rs2", [P, 4, T])
        x2 = pair_of("x2", [P, T, D])
        x2_t = pair_of("x2_t", [P, T * P])
        lo8 = pair_of("lo8", [P, T, E])
        eq8 = pair_of("eq8", [P, T, E])
        ky8 = pair_of("ky8", [P, T, E])
        l28 = pair_of("l28", [P, T, E])
        m4 = pair_of("m4", [P, 6, T])
        e4 = pair_of("e4", [P, T])
        w4 = pair_of("w4", [P, 6, T])
        pick = pair_of("pick", [P, T, NPAIR], BF16)
        picked = pair_of("picked", [P, T, NPAIR])
        slot_f = pair_of("slot_f", [P, T])
        slot = pair_of("slot", [P, T], I32)
        tid = pair_of("tid", [P, T], I32)

        base_all = sb("base_all", [P, NPAIR])
        rest_no = sb("rest_no", [P, 1])
        any_pair = sb("any_pair", [P, 1])
        tab_cols = sb("tab_cols", [P, 3])
        cnt_i = sb("cnt_i", [P, 2, NPAIR], I32)
        n_full = sb("n_full", [P, NPAIR])
        ends = sb("ends", [P, NPAIR])
        starts = sb("starts", [P, NPAIR])
        inside = sb("inside", [P, 4, NPAIR])
        row_of = sb("row_of", [P, NPAIR])
        vals = sb("vals", [P, 5])
        tile_row = sb("tile_row", [P, 4])
        prod = sb("prod", [P, 5, NPAIR])
        ones_pair = sb("ones_pair", [P, NPAIR])
        rest_of = sb("rest_of", [P, NPAIR])
        rest_row = sb("rest_row", [P, NPAIR])
        table = sb("table", [1, P, 3], I32)
        pad_row = sb("pad_row", [1, NPAIR], I32)

        token = [sb(f"token{i}", [P, 1], I32) for i in range(4)]
        w_two = [sb(f"w_two{i}", [P, 2, 4, H], F16) for i in range(4)]
        b_two = [sb(f"b_two{i}", [P, 2, H + D], BF16) for i in range(4)]
        tn = pair_of("tn", [P, D])
        th = pair_of("th", [P, P], F16)
        tl = pair_of("tl", [P, P], F16)
        hh = pair_of("hh", [P, 2 * HC * P], F16)
        hl = pair_of("hl", [P, 2 * HC * P], F16)
        ya = pair_of("ya", [P, D])
        yb = pair_of("yb", [P, D])
        yo = [sb(f"yo{i}", [P, D]) for i in range(4)]

        bank_a = [bank("bank_a0"), bank("bank_a1")]
        bank_x = bank("bank_x")
        bank_z = bank("bank_z")
        bank_p = bank("bank_p")
        bank_g = bank("bank_g")
        bank_l = bank("bank_l")
        bank_r = bank("bank_r")
        logits_p = bank_l[:, 0:T * E]
        rank_p = bank_r[:, 0:T * NPAIR]
        bank_t, bank_h, bank_y = [bank_x, bank_z], bank_a, [bank_p, bank_g]

        consts_in, weights_in = sem("consts_in"), sem("weights_in")
        adj_in, x_in, xr_in = sem2("adj_in"), sem2("x_in"), sem2("xr_in")
        scattered = sem2("scattered")
        bias_out, bias_placed = sem("bias_out"), sem("bias_placed")
        pads_out = sem("pads_out")
        tile_loaded = [sem(f"tile_loaded{i}") for i in range(4)]
        stored = [sem(f"stored{i}") for i in range(4)]
        pool_c, dve_c, act_c, peak_ready = sem("pool_c"), sem("dve_c"), sem("act_c"), sem("peak_ready")
        var_ready, y_ready = sem("var_ready"), sem("y_ready")
        u_ready, ug_ready, xn_ready = sem("u_ready"), sem("ug_ready"), sem("xn_ready")
        xn_t_made, xn_t_ready = sem("xn_t_made"), sem("xn_t_ready")
        adj_t_made, adj_t_ready = sem("adj_t_made"), sem("adj_t_ready")
        deg_ready, degy_ready, sxn_ready = sem("deg_ready"), sem("degy_ready"), sem("sxn_ready")
        z_made, z_ready, p_made, p_ready = sem("z_made"), sem("z_ready"), sem("p_made"), sem("p_ready")
        g_made, pre_ready, lg_ready, sp_ready = sem("g_made"), sem("pre_ready"), sem("lg_ready"), sem("sp_ready")
        x1_ready, var2_ready, y2_ready, x2_ready = sem("x1_ready"), sem("var2_ready"), sem("y2_ready"), sem("x2_ready")
        x2_t_made, x2_t_ready = sem("x2_t_made"), sem("x2_t_ready")
        logits_made, logits_read, gap_ready, e_ready = sem("logits_made"), sem("logits_read"), sem("gap_ready"), sem("e_ready")
        row_ready, pick_ready, rank_made, slot_ready = sem("row_ready"), sem("pick_ready"), sem("rank_made"), sem("slot_ready")
        pay_ready, sdeg_ready, norm2_ready, dve9 = sem("pay_ready"), sem("sdeg_ready"), sem("norm2_ready"), sem("dve9")
        degc_ready, w_ready, counted = sem("degc_ready"), sem("w_ready"), sem("counted")
        dve1, dve2, dve3, dve4, dve5, dve6, dve7, dve8 = (sem(f"dve{i}") for i in range(1, 9))
        act1, act2, act3, act4 = (sem(f"act{i}") for i in range(1, 5))
        pool2, pool3 = sem("pool2"), sem("pool3")
        count_made, tab_steps, tab_ready, tab_t, tab_row = (
            sem("count_made"), sem("tab_steps"), sem("tab_ready"), sem("tab_t"), sem("tab_row"))
        w_placed, b_placed = sem("w_placed"), sem("b_placed")
        tn_ready, t_made, th_ready, tl_ready = sem("tn_ready"), sem("t_made"), sem("th_ready"), sem("tl_ready")
        h_made, hh_ready, hl_ready = sem("h_made"), sem("hh_ready"), sem("hl_ready")
        y_made, ya_ready, yb_ready, yo_ready = sem("y_made"), sem("ya_ready"), sem("yb_ready"), sem("yo_ready")

        class Item:

            def __init__(self, n, par, turn, slot):
                self.n, self.par, self.turn, self.slot = n, par, turn, slot

        def item(n, unroll=2):
            return Item(n, n % 2, n // unroll, n % unroll)

        def pipeline(eng, count, stages, step, unroll=2, between=None, begin=None):
            def at(i):
                return item(i, unroll) if 0 <= i < count else None

            peeled = -(-(stages - 1 + unroll) // unroll) * unroll
            for i in range(peeled):
                if begin and i % unroll == 0:
                    begin(i)
                step(*[at(i - j) for j in range(stages)])
                if between:
                    between(i)
            with eng.Fori(peeled // unroll, count // unroll) as turn:
                if begin:
                    begin(turn * unroll)
                for i in range(unroll):
                    step(*[Item(turn * unroll + (i - j), (i - j) % 2, turn + (i - j) // unroll, (i - j) % unroll)
                           for j in range(stages)])
            for i in range(count, count + stages - 1):
                if begin and i % unroll == 0:
                    begin(i)
                step(*[at(i - j) for j in range(stages)])

        def after(eng, signal, value):
            if not isinstance(value, int) or value > 0:
                eng.wait_ge(signal, value)

        def apart(eng, met, signal, value):
            if not isinstance(value, int):
                value = eng.to_reg(value)
            eng.wait_ge(*met)
            eng.wait_ge(signal, value)

        class Steps:

            def __init__(self, eng, own, n, per):
                self.eng, self.own, self.base, self.per, self.n = eng, own, n * per, per, 0

            def then(self, ins, met=None):
                self.n += 1
                assert self.n <= self.per
                ins.then_inc(self.own, 1)
                if met:
                    apart(self.eng, met, self.own, self.base + self.n)
                else:
                    self.eng.wait_ge(self.own, self.base + self.n)

            def close(self):
                assert self.n == self.per, (self.n, self.per)

        def each(ap, n):
            return ap.unsqueeze(2).broadcast_to([P, T, n])

        def per_tile(ap, n):
            return ap.unsqueeze(1).broadcast_to([P, T, n])

        U = 4
        POOL_BLANK, POOL_ALL = 6, 19
        DVE_GATE, DVE_PEAK, DVE_BIAS, DVE_ALL = 2, 4, 4 + 12, 4 + 12 + 2
        ACT_W = 2

        PLACE = 2

        def expert_numbers(eng, i):
            first, count = i - PLACE, U
            if isinstance(i, int):
                first, count = max(first, 0), min(i - PLACE + U, TILES) - max(first, 0)
            _, numbers = nc.values_load_multi_w_load_instructions(
                table[0:1, bass.ds(first, count), 1:3], engines=[eng.engine], min_val=0, max_val=E - 1,
                skip_runtime_bounds_check_because="the table was made with numbers of experts alone")
            slot = first % U if isinstance(i, int) else -PLACE % U
            return {(slot + k) % U: numbers[2 * k:2 * k + 2] for k in range(count)}

        block = ctx.enter_context(nc.Block())

        @block.sync
        def _(sp_e):
            def load_graph(g):
                after(sp_e, adj_t_made, T * (g.n - 1))
                after(sp_e, deg_ready, g.n - 1)
                sp_e.dma_start(adj_s[g.par][:], adj_v[g.n]).then_inc(adj_in[g.par], 16)
                after(sp_e, u_ready, g.n - 1)
                sp_e.dma_start(x_s[g.par][:], x_v[g.n]).then_inc(x_in[g.par], 16)

            def load_again(g):
                after(sp_e, x1_ready, g.n - 1)
                sp_e.dma_start(xr_s[g.par][:], x_v[g.n]).then_inc(xr_in[g.par], 16)

            def load(g0, g1):
                if g0:
                    load_graph(g0)
                if g1:
                    load_again(g1)

            def load_rest(i):
                if i == 0:
                    for dst, src in ((gamma_b[:], gamma.partition_broadcast(P)), (beta_b[:], beta.partition_broadcast(P)),
                                     (w_self_s[:], w_self), (w_neigh_s[:], w_neigh), (w_gate_s[:], w_gate),
                                     (gate_row[:, 0, :], b_gate.unsqueeze(0)),
                                     (gate_row[:, 1, :], bias_gate.unsqueeze(0))):
                        sp_e.dma_start(dst, src).then_inc(consts_in, 16)
                if i == 1:
                    b1_v = b1.rearrange("e h -> (e h)").rearrange("(p c) -> p c", p=P)
                    b2_v = b2.rearrange("e d -> (e d)").rearrange("(p c) -> p c", p=P)
                    for dst, src in ((w1f[:], w1.rearrange("e d h -> d e h")),
                                     (w2f[:], w2.rearrange("e (c h) d -> h e c d", h=P)),
                                     (bv[:, 0:NB1], b1_v), (bv[:, NB1:NB1 + NB2], b2_v)):
                        sp_e.dma_start(dst, src).then_inc(weights_in, 16)
                    sp_e.wait_ge(pool_c, POOL_BLANK)
                    sp_e.dma_start(sorted_rows[DUMMY:DUMMY + P, :], blank_rows[:]).then_inc(pads_out, 16)

            pipeline(sp_e, B, 2, load, between=load_rest)

            sp_e.wait_ge(pool_c, POOL_ALL)
            sp_e.wait_ge(dve_c, DVE_BIAS)
            sp_e.dma_start(b1_parts.rearrange("s (p c) -> p s c", p=P), bpart[:, :, 0:NB1]).then_inc(bias_out, 16)
            sp_e.dma_start(b2_parts.rearrange("s (p c) -> p s c", p=P), bpart[:, :, NB1:NB1 + NB2]).then_inc(bias_out, 16)
            sp_e.wait_ge(bias_out, 16 * 2)
            sp_e.dma_start(b_all[0:3, :, 0:H], b1_parts.rearrange("s (e h) -> s e h", e=E)).then_inc(bias_placed, 16)
            sp_e.dma_start(b_all[0:3, :, H:H + D], b2_parts.rearrange("s (e h) -> s e h", e=E)).then_inc(bias_placed, 16)

            sp_e.wait_ge(tab_ready, 2)
            for par in range(2):
                sp_e.wait_ge(scattered[par], 16 * T * TURNS)
            sp_e.wait_ge(pads_out, 16)

            def load_tile(g):
                row = sp_e.value_load(table[0:1, bass.ds(g.n, 1), 0], min_val=0, max_val=DUMMY)
                after(sp_e, tile_loaded[g.slot], 16 * g.turn)
                sp_e.wait_ge(tab_ready, 2)
                sp_e.dma_start(rows_in[:, bass.ds(g.n, 1), :].rearrange("p a d -> p (a d)"),
                               sorted_rows[bass.ds(row, P), :]).then_inc(tile_loaded[g.slot], 16)

            def pad(q):
                row = sp_e.value_load(pad_row[0:1, bass.ds(q, 1)], min_val=0, max_val=DUMMY)
                sp_e.dma_start(sorted_rows[bass.ds(row, P), :], blank_rows[:]).then_inc(pads_out, 16)

            for i in range(U):
                load_tile(item(i, U))
            with sp_e.Fori(1, FULL // U) as turn:
                for i in range(U):
                    load_tile(Item(turn * U + i, i % 2, turn, i))
            with sp_e.Fori(0, NPAIR) as q:
                pad(q)
            sp_e.wait_ge(pads_out, 16 * (NPAIR + 1))
            with sp_e.Fori(FULL // U, TILES // U) as turn:
                for i in range(U):
                    load_tile(Item(turn * U + i, i % 2, turn, i))
            for i in range(U):
                sp_e.wait_ge(stored[i], 16 * (TILES // U))

        @block.gpsimd
        def _(pool):
            count = [0]

            def made(ins, wait=False):
                count[0] += 1
                ins.then_inc(pool_c, 1)
                if wait:
                    pool.wait_ge(pool_c, count[0])

            made(pool.memset(ident[:], 0.0), True)
            made(pool.affine_select(out=ident[:], in_=ident[:], compare_op=ALU.not_equal, fill=1.0, base=0,
                                    pattern=[[-1, P]], channel_multiplier=1))
            made(pool.memset(one_row[:], 1.0))
            made(pool.memset(blank_rows[:], 0.0), True)
            made(pool.memset(blank_rows[:, TOKEN:TOKEN + 1].bitcast(I32), SKIPPED))
            made(pool.memset(zero4[:], 0))
            assert count[0] == POOL_BLANK

            def constants(i):
                if i != 0:
                    return
                made(pool.memset(step4[:], 2 * N))
                for par in range(2):
                    made(pool.memset(pay[par][:], 0.0))
                    made(pool.iota(tid[par][:], [[P, T]], base=par * N, channel_multiplier=1,
                                   allow_small_or_imprecise_dtypes=True))
                pool.wait_ge(pool_c, count[0])
                pool.memset(ones_pair[:], 1.0)
                pool.memset(zero_i[:], 0)
                pool.memset(zero_bf[:], 0.0)
                pool.memset(p_row[:], float(P))
                pool.memset(ones_bf[:], 1.0)
                made(pool.memset(b_all[:], 0.0))
                made(pool.memset(before[:], 1.0))
                made(pool.memset(upto[:], 1.0), True)
                made(pool.affine_select(out=before[:], in_=before[:], compare_op=ALU.is_gt, fill=0.0, base=0,
                                        pattern=[[1, P]], channel_multiplier=-1))
                made(pool.affine_select(out=upto[:], in_=upto[:], compare_op=ALU.is_ge, fill=0.0, base=0,
                                        pattern=[[-1, P]], channel_multiplier=1))
                for e in range(E):
                    pool.memset(rev[:, e:e + 1], float(2 ** (E - 1 - e)))
                for q, (a, b) in enumerate(PAIRS):
                    pool.memset(codes[:, q:q + 1], float(2 ** (E - 1 - a) + 2 ** (E - 1 - b)))
                    pool.memset(pair_a[:, q:q + 1], float(a))
                    pool.memset(pair_b[:, q:q + 1], float(b))
                made(pool.iota(pair_base[:], [[0, T], [REGION // P, NPAIR]], base=0, channel_multiplier=0,
                               allow_small_or_imprecise_dtypes=True))
                made(pool.iota(pair_base_all[:], [[REGION // P, NPAIR]], base=0, channel_multiplier=0,
                               allow_small_or_imprecise_dtypes=True))
                made(pool.iota(tile_no[:], [[0, 1]], base=0, channel_multiplier=1,
                               allow_small_or_imprecise_dtypes=True))
                assert count[0] == POOL_ALL, count

            def affine(g):
                pool.wait_ge(u_ready, g.n + 1)
                after(pool, xn_t_made, g.n - 1)
                after(pool, sxn_ready, g.n - 1)
                pool.tensor_tensor(xn_s[g.par][:], u_s[g.par][:], per_tile(gamma_b[:], D),
                                   ALU.mult).then_inc(ug_ready, 1)
                pool.wait_ge(ug_ready, g.n + 1)
                pool.tensor_tensor(xn_s[g.par][:], xn_s[g.par][:], per_tile(beta_b[:], D),
                                   ALU.add).then_inc(xn_ready, 1)

            def residual(g):
                pool.wait_ge(sp_ready, g.n + 1)
                pool.wait_ge(xr_in[g.par], 16 * (g.turn + 1))
                after(pool, scattered[g.par], 16 * T * g.turn)
                pool.tensor_tensor(pay[g.par][:, :, 0:D], sp[g.par][:], xr_s[g.par][:], ALU.add).then_inc(x1_ready, 1)
                s = Steps(pool, pool2, g.n, 2)
                s.then(pool.tensor_tensor(pay[g.par][:, :, TOKEN].bitcast(I32), tid[g.par][:], zero4[:], ALU.add))
                s.then(pool.tensor_tensor(tid[g.par][:], tid[g.par][:], step4[:], ALU.add))
                s.close()

            def weights(g):
                w = w4[g.par]
                s = Steps(pool, pool3, g.n, 4)
                pool.wait_ge(w_ready, g.n + 1)
                s.then(pool.tensor_tensor(w[:, 2, :], w[:, 1, :], e4[g.par][:], ALU.mult))
                s.then(pool.tensor_tensor(w[:, 3, :], w[:, 1, :], w[:, 2, :], ALU.subtract))
                s.then(pool.tensor_tensor(w[:, 5, :], w[:, 3, :], w[:, 4, :], ALU.mult))
                s.then(pool.tensor_tensor(pay[g.par][:, :, WA], w[:, 2, :], w[:, 5, :], ALU.add))
                pool.tensor_tensor(pay[g.par][:, :, WA + 1], w[:, 1, :], w[:, 5, :],
                                   ALU.subtract).then_inc(pay_ready, 1)
                s.close()

            def scatter(g):
                n = g.n + 1 if isinstance(g.n, int) else pool.to_reg(g.n + 1)
                pool.wait_ge(pool_c, POOL_ALL)
                pool.wait_ge(pay_ready, n)
                pool.wait_ge(slot_ready, n)
                for t in range(T):
                    pool.indirect_dma_start(
                        sorted_rows[:, :], bass.IndirectOffsetOnAxis(ap=slot[g.par][:, t:t + 1], axis=0),
                        pay[g.par][:, t, :], None).then_inc(scattered[g.par], 16)

            def graphs(g0, g1, g2, g3):
                if g2:
                    residual(g2)
                if g3:
                    weights(g3)
                if g0:
                    affine(g0)
                if g3:
                    scatter(g3)

            def between(i):
                constants(i)
                if i == 1:
                    pool.wait_ge(dve_c, DVE_PEAK)
                    pool.partition_all_reduce(peak_all[:], peak2[:], P, RMAX).then_inc(peak_ready, 1)

            pool.wait_ge(consts_in, 16 * 7)
            pipeline(pool, B, 4, graphs, between=between)

            def finish(g):
                pool.wait_ge(yb_ready, g.n + 1)
                after(pool, stored[g.slot], 16 * g.turn)
                pool.wait_ge(pool_c, POOL_ALL)
                row = rows_in[:, bass.ds(g.n, 1), :].rearrange("p a d -> p (a d)")
                pool.tensor_tensor(yo[g.slot][:], yb[g.par][:], row[:, 0:D], ALU.add)
                pool.tensor_tensor(token[g.slot][:], row[:, TOKEN:TOKEN + 1].bitcast(I32), zero_i[:],
                                   ALU.add).then_inc(yo_ready, 1)
                apart(pool, (pool_c, POOL_ALL), yo_ready, g.n + 1)
                pool.indirect_dma_start(
                    out_rows, bass.IndirectOffsetOnAxis(ap=token[g.slot][:], axis=0),
                    yo[g.slot][:], None, bounds_check=TOKENS - 1, oob_is_err=False).then_inc(stored[g.slot], 16)

            pipeline(pool, TILES, 1, finish, unroll=U)

        @block.scalar
        def _(act):
            act.preload_act_table_set("natural_log_exp_and_others")

            def root(dst, src, n):
                act.activation(dst[1], src, ACT.Ln).then_inc(n[0], 1)
                act.wait_ge(n[0], n[1])
                return act.activation(dst[0], dst[1], ACT.Exp, scale=-0.5)

            def first_guess(g):
                act.wait_ge(var_ready, g.n + 1)
                r = rs[g.par]
                root((r[:, 1, :], r[:, 2, :]), r[:, 0, :], (act1, g.n + 1)).then_inc(y_ready, 1)

            def sum_rows(g):
                act.wait_ge(adj_in[g.par], 16 * (g.turn + 1))
                after(act, sdeg_ready, g.n - 1)
                for t in range(T):
                    last = act.activation(junk[:, t, :], adj_s[g.par][:, t, :], ACT.Copy,
                                          accum_out=deg[g.par][:, 0, t:t + 1])
                last.then_inc(deg_ready, 1)

            def evacuate(g, t):
                act.wait_ge(adj_t_made, T * g.n + t + 1)
                if t == 0:
                    after(act, z_made, g.n - 1)
                act.activation(adj_t[g.par][:, t, :], bank_a[t % 2][:], ACT.Copy,
                               accum_out=deg[g.par][:, 1, t:t + 1]).then_inc(adj_t_ready, 1)

            def degree_guess(g):
                act.wait_ge(degc_ready, g.n + 1)
                d = deg_w[g.par]
                root((d[:, 0], d[:, 1]), deg_c[g.par][:], (act2, g.n + 1)).then_inc(degy_ready, 1)

            def xn_out(g):
                act.wait_ge(xn_t_made, g.n + 1)
                after(act, p_made, g.n - 1)
                act.activation(xn_t[g.par][:], bank_x[:], ACT.Copy).then_inc(xn_t_ready, 1)

            def scale_xn(g):
                act.wait_ge(sdeg_ready, g.n + 1)
                act.wait_ge(xn_ready, g.n + 1)
                after(act, z_made, g.n - 1)
                for t in range(T):
                    last = act.activation(sxn[g.par][:, t, :], xn_s[g.par][:, t, :], ACT.Copy,
                                          scale=s_deg[g.par][:, 0, t:t + 1])
                last.then_inc(sxn_ready, 1)

            def p_out(g):
                act.wait_ge(p_made, g.n + 1)
                after(act, pre_ready, g.n - 1)
                act.activation(p_s[g.par][:], bank_p[:], ACT.Copy).then_inc(p_ready, 1)

            def z_out(g):
                act.wait_ge(z_made, g.n + 1)
                after(act, g_made, g.n - 1)
                act.activation(z_t[g.par][:, 0, :], bank_z[:], ACT.Copy).then_inc(z_ready, 1)

            def softplus(g):
                act.wait_ge(pre_ready, g.n + 1)
                after(act, x1_ready, g.n - 1)
                act.activation(pre_c[g.par][:], pre_c[g.par][:], ACT.Exp).then_inc(act3, 1)
                act.wait_ge(act3, g.n + 1)
                act.activation(sp[g.par][:].rearrange("p t d -> p (t d)"), pre_c[g.par][:], ACT.Ln, bias=1.0).then_inc(lg_ready, 1)

            def second_guess(g):
                act.wait_ge(var2_ready, g.n + 1)
                r = rs2[g.par]
                root((r[:, 1, :], r[:, 2, :]), r[:, 0, :], (act4, g.n + 1)).then_inc(y2_ready, 1)

            def second_normalise(g):
                act.wait_ge(norm2_ready, g.n + 1)
                after(act, x2_t_made, g.n - 1)
                for t in range(T):
                    last = act.activation(x2[g.par][:, t, :], pay[g.par][:, t, 0:D], ACT.Identity,
                                          bias=shift2[g.par][:, t:t + 1], scale=pay[g.par][:, t, RSTD:RSTD + 1])
                last.then_inc(x2_ready, 1)

            def x2_out(g):
                act.wait_ge(x2_t_made, g.n + 1)
                act.activation(x2_t[g.par][:], bank_x[:], ACT.Copy).then_inc(x2_t_ready, 1)

            def gate_exp(g):
                act.wait_ge(gap_ready, g.n + 1)
                after(act, pay_ready, g.n - 1)
                act.activation(e4[g.par][:], m4[g.par][:, 4, :], ACT.Exp).then_inc(e_ready, 1)

            def graphs(g0, g1, g2, g3):
                if g2:
                    softplus(g2)
                if g1:
                    xn_out(g1)
                if g3:
                    gate_exp(g3)
                if g1:
                    scale_xn(g1)
                if g0:
                    sum_rows(g0)
                    first_guess(g0)
                if g2:
                    second_guess(g2)
                if g0:
                    evacuate(g0, 0)
                if g1:
                    p_out(g1)
                    z_out(g1)
                if g2:
                    second_normalise(g2)
                if g0:
                    evacuate(g0, 1)
                    evacuate(g0, 2)
                if g2:
                    x2_out(g2)
                if g0:
                    evacuate(g0, 3)
                    degree_guess(g0)

            def between(i):
                if i == 2:
                    act.wait_ge(weights_in, 16 * 4)
                    act.wait_ge(dve_c, DVE_BIAS)
                    act.activation(w_all[:, :, 0, :], w1f[:], ACT.Copy,
                                   scale=scale_f[:, 0:1]).then_inc(act_c, 1)
                    act.activation(w_all[:, :, 2, :], w2f[:].rearrange("p e c d -> p e (c d)"), ACT.Copy,
                                   scale=scale_f[:, 1:2]).then_inc(act_c, 1)

            pipeline(act, B, 4, graphs, between=between)

            experts = {}

            def load_experts(n):
                experts.update(expert_numbers(act, n))

            def place_biases(g):
                after(act, y_made, g.n - (U - 1))
                for k, e in enumerate(experts[g.slot]):
                    ins = act.activation(b_two[g.slot][:, k], b_all[:, bass.ds(e, 1), :].rearrange("p e h -> p (e h)"), ACT.Copy)
                ins.then_inc(b_placed, 1)

            def lead_x(g):
                act.wait_ge(t_made, g.n + 1)
                act.activation(th[g.par][:], bank_t[g.par][:, 0:P], ACT.Copy).then_inc(th_ready, 1)

            def lead_h(g):
                act.wait_ge(h_made, g.n + 1)
                after(act, y_made, g.n - 1)
                act.activation(hh[g.par][:], bank_h[g.par][:], ACT.Relu).then_inc(hh_ready, 1)

            def first_expert(g):
                act.wait_ge(y_made, g.n + 1)
                after(act, yb_ready, g.n - 1)
                act.wait_ge(dve_c, DVE_ALL)
                row = rows_in[:, bass.ds(g.n, 1), :].rearrange("p a d -> p (a d)")
                act.activation(ya[g.par][:], bank_y[g.par][:, 0:D], ACT.Copy,
                               scale=row[:, WA:WA + 1]).then_inc(ya_ready, 1)

            def tiles(g0, g1, g2, g3, g4, g5, g6):
                if g4:
                    lead_h(g4)
                if g2:
                    lead_x(g2)
                if g2:
                    place_biases(g2)
                if g6:
                    first_expert(g6)

            act.wait_ge(tab_ready, 2)
            act.wait_ge(bias_placed, 16 * 2)
            pipeline(act, TILES, 7, tiles, unroll=U, begin=load_experts)

        @block.vector
        def _(dve):
            count = [0]

            def made(ins, wait=True):
                count[0] += 1
                ins.then_inc(dve_c, 1)
                if wait:
                    dve.wait_ge(dve_c, count[0])

            def newton(s, r, arg, y, t1, t2, dst):
                s.then(dve.scalar_tensor_tensor(out=t1, in0=y, scalar=-0.5, in1=arg, op0=ALU.mult, op1=ALU.mult))
                s.then(dve.tensor_tensor(t2, t1, y, ALU.mult))
                s.then(dve.scalar_tensor_tensor(out=dst, in0=t2, scalar=1.5, in1=y, op0=ALU.add, op1=ALU.mult))

            def statistics(g):
                dve.wait_ge(x_in[g.par], 16 * (g.turn + 1))
                s = Steps(dve, dve1, g.n, 2)
                for t in range(T):
                    last = dve.bn_stats(st[g.par][:, t, :], x_s[g.par][:, t, :])
                s.then(last, met=(pool_c, 1))
                for t in range(T):
                    last = dve.bn_aggr(mv[g.par][:, t, :], st[g.par][:, t, :])
                s.then(last)
                s.close()
                dve.tensor_scalar(rs[g.par][:, 0, :], mv[g.par][:, :, 1], 1.0 + EPS, EPS * EPS,
                                  ALU.mult, ALU.add).then_inc(var_ready, 1)

            def normalise(g):
                dve.wait_ge(y_ready, g.n + 1)
                r = rs[g.par]
                s = Steps(dve, dve2, g.n, 3)
                newton(s, r, r[:, 0, :], r[:, 1, :], r[:, 2, :], r[:, 3, :], rstd[g.par][:])
                s.close()
                after(dve, ug_ready, g.n - 1)
                for t in range(T):
                    last = dve.tensor_scalar(u_s[g.par][:, t, :], x_s[g.par][:, t, :], mv[g.par][:, t, 0:1],
                                             rstd[g.par][:, t:t + 1], ALU.subtract, ALU.mult)
                last.then_inc(u_ready, 1)

            def degrees(g):
                dve.wait_ge(deg_ready, g.n + 1)
                dve.wait_ge(adj_t_ready, T * (g.n + 1))
                dve.tensor_scalar(deg_c[g.par][:], deg[g.par][:], 1e-18, None, ALU.max).then_inc(degc_ready, 1)

            def scale_rows(g):
                dve.wait_ge(degy_ready, g.n + 1)
                after(dve, sxn_ready, g.n - 1)
                d = deg_w[g.par]
                s = Steps(dve, dve3, g.n, 5)
                newton(s, None, deg_c[g.par][:], d[:, 0], d[:, 1], d[:, 2], d[:, 3])
                s.then(dve.tensor_scalar(d[:, 1], deg[g.par][:], 0.0, None, ALU.not_equal))
                s.then(dve.tensor_tensor(s_deg[g.par][:], d[:, 3], d[:, 1], ALU.mult))
                s.close()
                dve.tensor_scalar(s_neg[g.par][:], s_deg[g.par][:, 1, :], -1.0, None, ALU.mult).then_inc(sdeg_ready, 1)

            def combine(g):
                dve.wait_ge(sdeg_ready, g.n + 1)
                dve.wait_ge(p_ready, g.n + 1)
                dve.wait_ge(g_made, g.n + 1)
                s = Steps(dve, dve4, g.n, 1)
                for t in range(T):
                    c = slice(t * D, (t + 1) * D)
                    last = dve.scalar_tensor_tensor(out=pre[g.par][:, c], in0=bank_g[:, c], scalar=s_neg[g.par][:, t:t + 1],
                                                    in1=p_s[g.par][:, c], op0=ALU.mult, op1=ALU.add)
                s.then(last)
                s.close()
                after(dve, lg_ready, g.n - 1)
                dve.tensor_scalar(pre_c[g.par][:], pre[g.par][:], 40.0, None, ALU.min).then_inc(pre_ready, 1)

            def soft(g):
                dve.wait_ge(lg_ready, g.n + 1)
                soft_s = sp[g.par][:].rearrange("p t d -> p (t d)")
                dve.tensor_tensor(soft_s, soft_s, pre[g.par][:], ALU.max).then_inc(sp_ready, 1)

            def second_norm(g):
                dve.wait_ge(x1_ready, g.n + 1)
                s = Steps(dve, dve5, g.n, 2)
                for t in range(T):
                    last = dve.bn_stats(st2[g.par][:, t, :], pay[g.par][:, t, 0:D])
                s.then(last, met=(pool_c, 1))
                for t in range(T):
                    last = dve.bn_aggr(mv2[g.par][:, t, :], st2[g.par][:, t, :])
                s.then(last)
                s.close()
                dve.tensor_scalar(rs2[g.par][:, 0, :], mv2[g.par][:, :, 1], EPS, None, ALU.add).then_inc(var2_ready, 1)

            def second_root(g):
                r = rs2[g.par]
                dve.wait_ge(y2_ready, g.n + 1)
                s = Steps(dve, dve6, g.n, 4)
                newton(s, r, r[:, 0, :], r[:, 1, :], r[:, 2, :], r[:, 3, :], pay[g.par][:, :, RSTD])
                s.then(dve.tensor_copy(pay[g.par][:, :, MEAN], mv2[g.par][:, :, 0]))
                s.close()
                dve.scalar_tensor_tensor(out=shift2[g.par][:], in0=mv2[g.par][:, :, 0], scalar=-1.0,
                                         in1=pay[g.par][:, :, RSTD], op0=ALU.mult, op1=ALU.mult).then_inc(norm2_ready, 1)

            def choose(g):
                i = g.par
                lo, eq, ky, l2, m = lo8[i][:], eq8[i][:], ky8[i][:], l28[i][:], m4[i]
                dve.wait_ge(logits_made, g.n + 1)
                after(dve, pay_ready, g.n - 1)
                after(dve, counted, g.n - 1)
                s = Steps(dve, dve7, g.n, 12)
                s.then(dve.tensor_copy(lo, logits_p))
                s.then(dve.tensor_reduce(m[:, 0, :], lo, AX_X, ALU.max))
                s.then(dve.tensor_tensor(eq, lo, each(m[:, 0, :], E), ALU.is_equal))
                s.then(dve.tensor_tensor(ky, eq, per_tile(rev[:], E), ALU.mult))
                s.then(dve.tensor_reduce(m[:, 1, :], ky, AX_X, ALU.max))
                s.then(dve.tensor_tensor(eq, per_tile(rev[:], E), each(m[:, 1, :], E), ALU.is_equal))
                s.then(dve.scalar_tensor_tensor(out=l2, in0=eq, scalar=-3.0e38, in1=lo, op0=ALU.mult, op1=ALU.add))
                s.then(dve.tensor_reduce(m[:, 2, :], l2, AX_X, ALU.max))
                dve.tensor_tensor(m[:, 4, :], m[:, 2, :], m[:, 0, :], ALU.subtract).then_inc(gap_ready, 1)
                s.then(dve.tensor_tensor(eq, l2, each(m[:, 2, :], E), ALU.is_equal))
                s.then(dve.tensor_tensor(ky, eq, per_tile(rev[:], E), ALU.mult))
                s.then(dve.tensor_reduce(m[:, 3, :], ky, AX_X, ALU.max))
                dve.tensor_tensor(w4[i][:, 4, :], m[:, 1, :], m[:, 3, :], ALU.is_gt)
                s.then(dve.tensor_tensor(m[:, 5, :], m[:, 1, :], m[:, 3, :], ALU.add))
                s.close()
                dve.tensor_tensor(pick[i][:], per_tile(codes[:], NPAIR), each(m[:, 5, :], NPAIR),
                                  ALU.is_equal).then_inc(pick_ready, 1)

            def share(g):
                w = w4[g.par]
                dve.wait_ge(e_ready, g.n + 1)
                s = Steps(dve, dve9, g.n, 2)
                s.then(dve.tensor_scalar(w[:, 0, :], e4[g.par][:], 1.0, None, ALU.add))
                s.then(dve.reciprocal(w[:, 5, :], w[:, 0, :]))
                s.close()
                dve.tensor_scalar(w[:, 1, :], w[:, 5, :], inv12[:], None, ALU.mult).then_inc(w_ready, 1)

            def place(g):
                i = g.par
                dve.wait_ge(rank_made, g.n + 1)
                after(dve, scattered[i], 16 * T * g.turn)
                s = Steps(dve, dve8, g.n, 2)
                s.then(dve.tensor_tensor(picked[i][:], rank_p, pick[i][:], ALU.mult))
                s.then(dve.tensor_reduce(slot_f[i][:], picked[i][:], AX_X, ALU.add))
                s.close()
                dve.tensor_copy(slot[i][:], slot_f[i][:]).then_inc(slot_ready, 1)

            def graphs(g0, g1, g2, g3):
                if g3:
                    choose(g3)
                if g1:
                    scale_rows(g1)
                if g2:
                    soft(g2)
                if g0:
                    statistics(g0)
                if g2:
                    second_norm(g2)
                if g3:
                    share(g3)
                if g2:
                    second_root(g2)
                if g0:
                    normalise(g0)
                if g3:
                    place(g3)
                if g1:
                    combine(g1)
                if g0:
                    degrees(g0)

            def between(i):
                if i == 0:
                    dve.wait_ge(weights_in, 16 * 4)
                    dve.tensor_reduce(peak[:, 1:2], bv[:, 0:NB1], AX_X, ALU.max, apply_absolute_value=True)
                    dve.tensor_reduce(peak2[:, 1:2], w2f[:].rearrange("p e c d -> p (e c d)"), AX_X, ALU.max,
                                      apply_absolute_value=True)
                    made(dve.tensor_reduce(peak[:, 0:1], w1f[:].rearrange("p e h -> p (e h)"), AX_X, ALU.max,
                                           apply_absolute_value=True))
                    made(dve.tensor_tensor(peak2[:, 0:1], peak[:, 0:1], peak[:, 1:2], ALU.max))
                    assert count[0] == DVE_PEAK
                if i == 1:
                    dve.wait_ge(peak_ready, 1)
                    made(dve.tensor_scalar(peak_c[:], peak_all[:], 1e-30, None, ALU.max))
                    made(dve.tensor_scalar(expo[:], peak_c[:].bitcast(I32), 0x7F800000, None, ALU.bitwise_and))
                    made(dve.tensor_scalar(scale_f[:].bitcast(I32), expo[:], -1.0, float(261 << 23), ALU.mult, ALU.add))
                    made(dve.tensor_scalar(inv_f[:].bitcast(I32), expo[:], float(7 << 23), None, ALU.subtract))
                    made(dve.tensor_tensor(scale12[:], scale_f[:, 0:1], scale_f[:, 1:2], ALU.mult))
                    made(dve.tensor_tensor(inv12[:], inv_f[:, 0:1], inv_f[:, 1:2], ALU.mult))
                    dve.tensor_scalar(brest[:, 0, 0:NB1], bv[:, 0:NB1], scale_f[:, 0:1], None, ALU.mult)
                    made(dve.tensor_scalar(brest[:, 0, NB1:NB1 + NB2], bv[:, NB1:NB1 + NB2], scale12[:], None, ALU.mult))
                    made(dve.tensor_copy(bpart[:, 0, :], brest[:, 0, :]))
                    made(dve.tensor_tensor(brest[:, 1, :], brest[:, 0, :], bpart[:, 0, :], ALU.subtract))
                    made(dve.tensor_copy(bpart[:, 1, :], brest[:, 1, :]))
                    made(dve.tensor_tensor(brest[:, 0, :], brest[:, 1, :], bpart[:, 1, :], ALU.subtract))
                    made(dve.tensor_copy(bpart[:, 2, :], brest[:, 0, :]))
                    assert count[0] == DVE_BIAS, count
                if i == 3:
                    dve.wait_ge(act_c, 2)
                    made(dve.scalar_tensor_tensor(out=w_all[:, :, 1, :], in0=w1f[:],
                                                  scalar=scale_f[:, 0:1], in1=w_all[:, :, 0, :], op0=ALU.mult, op1=ALU.subtract), False)
                    made(dve.scalar_tensor_tensor(out=w_all[:, :, 3, :], in0=w2f[:].rearrange("p e c d -> p e (c d)"),
                                                  scalar=scale_f[:, 1:2], in1=w_all[:, :, 2, :],
                                                  op0=ALU.mult, op1=ALU.subtract), False)
                    assert count[0] == DVE_ALL

            dve.wait_ge(consts_in, 16 * 7)
            made(dve.tensor_tensor(w_sum[:], w_self_s[:], w_neigh_s[:], ALU.add))
            made(dve.tensor_tensor(gate_bias[:], gate_row[:, 0, :].unsqueeze(1).broadcast_to([1, T, E]),
                                   gate_row[:, 1, :].unsqueeze(1).broadcast_to([1, T, E]), ALU.add))
            assert count[0] == DVE_GATE
            pipeline(dve, B, 4, graphs, between=between)

            tab = [0]

            def step(ins):
                tab[0] += 1
                ins.then_inc(tab_steps, 1)
                dve.wait_ge(tab_steps, tab[0])

            dve.wait_ge(count_made, 1)
            step(dve.tensor_scalar(base_all[:], pair_base_all[:], float(P), None, ALU.mult))
            step(dve.tensor_copy(pad_row[:], rank_p[0:1, 0:NPAIR]))
            step(dve.tensor_tensor(cnt_i[:, 0, :], rank_p[:, 0:NPAIR], base_all[:], ALU.subtract))
            step(dve.tensor_scalar(cnt_i[:, 1, :], cnt_i[:, 0, :], 7, None, ALU.logical_shift_right))
            step(dve.tensor_copy(n_full[:], cnt_i[:, 1, :]))
            step(dve.tensor_tensor_scan(ends[:], ones_pair[:], n_full[:], 0.0, ALU.mult, ALU.add))
            step(dve.tensor_tensor(starts[:], ends[:], n_full[:], ALU.subtract))
            step(dve.tensor_scalar(inside[:, 0, :], starts[:], tile_no[:], None, ALU.is_le))
            step(dve.tensor_scalar(inside[:, 1, :], ends[:], tile_no[:], None, ALU.is_gt))
            step(dve.tensor_tensor(inside[:, 2, :], inside[:, 0, :], inside[:, 1, :], ALU.mult))
            step(dve.tensor_scalar(rest_no[:], tile_no[:], -float(FULL), float(REGION // P), ALU.add, ALU.mult))
            step(dve.tensor_scalar(rest_of[:], pair_base_all[:], rest_no[:], None, ALU.is_equal))
            step(dve.tensor_tensor(inside[:, 3, :], inside[:, 2, :], rest_of[:], ALU.add))
            step(dve.scalar_tensor_tensor(out=row_of[:], in0=starts[:], scalar=-float(P), in1=base_all[:],
                                          op0=ALU.mult, op1=ALU.add))
            step(dve.scalar_tensor_tensor(out=rest_row[:], in0=n_full[:], scalar=float(P), in1=base_all[:],
                                          op0=ALU.mult, op1=ALU.add))
            step(dve.tensor_tensor(prod[:, 0, :], inside[:, 2, :], row_of[:], ALU.mult))
            step(dve.tensor_tensor(prod[:, 1, :], rest_of[:], rest_row[:], ALU.mult))
            step(dve.tensor_tensor(prod[:, 2, :], inside[:, 3, :], pair_a[:], ALU.mult))
            step(dve.tensor_tensor(prod[:, 3, :], inside[:, 3, :], pair_b[:], ALU.mult))
            step(dve.tensor_copy(prod[:, 4, :], inside[:, 2, :]))
            step(dve.tensor_reduce(vals[:], prod[:], AX_X, ALU.add))
            step(dve.tensor_reduce(any_pair[:], inside[:, 3, :], AX_X, ALU.add))
            step(dve.tensor_scalar(tile_row[:, 0:1], tile_no[:], float(P), None, ALU.mult))
            step(dve.tensor_tensor(tile_row[:, 1:2], tile_row[:, 0:1], vals[:, 4:5], ALU.mult))
            step(dve.tensor_scalar(tile_row[:, 2:3], any_pair[:], -float(DUMMY), float(DUMMY), ALU.mult, ALU.add))
            step(dve.scalar_tensor_tensor(out=tile_row[:, 3:4], in0=tile_row[:, 1:2], scalar=vals[:, 0:1],
                                          in1=tile_row[:, 2:3], op0=ALU.add, op1=ALU.add))
            step(dve.tensor_tensor(vals[:, 1:2], tile_row[:, 3:4], vals[:, 1:2], ALU.add))
            dve.tensor_copy(tab_cols[:], vals[:, 1:4]).then_inc(tab_ready, 1)
            dve.wait_ge(tab_t, 1)
            dve.tensor_copy(table[:].rearrange("p n c -> p c n"), bank_z[0:1, 0:3 * P].rearrange("p (c n) -> p c n", c=3)).then_inc(tab_ready, 1)

            def normal_row(g):
                dve.wait_ge(tile_loaded[g.slot], 16 * (g.turn + 1))
                after(dve, t_made, g.n - 1)
                row = rows_in[:, bass.ds(g.n, 1), :].rearrange("p a d -> p (a d)")
                dve.tensor_scalar(tn[g.par][:], row[:, 0:D], row[:, MEAN:MEAN + 1], row[:, RSTD:RSTD + 1],
                                  ALU.subtract, ALU.mult).then_inc(tn_ready, 1)

            experts = {}

            def load_experts(n):
                experts.update(expert_numbers(dve, n))

            def place_weights(g):
                after(dve, y_made, g.n - (U - 1))
                for k, e in enumerate(experts[g.slot]):
                    ins = dve.tensor_copy(w_two[g.slot][:, k].rearrange("p i h -> p (i h)"),
                                          w_all[:, bass.ds(e, 1), :, :].rearrange("p e i h -> p (e i h)"))
                ins.then_inc(w_placed, 1)

            def rest_x(g):
                dve.wait_ge(th_ready, g.n + 1)
                dve.tensor_tensor(tl[g.par][:], bank_t[g.par][:, 0:P], th[g.par][:], ALU.subtract).then_inc(tl_ready, 1)

            def rest_h(g):
                dve.wait_ge(hh_ready, g.n + 1)
                dve.scalar_tensor_tensor(out=hl[g.par][:], in0=bank_h[g.par][:], scalar=0.0, in1=hh[g.par][:],
                                         op0=ALU.max, op1=ALU.subtract).then_inc(hl_ready, 1)

            def both_experts(g):
                dve.wait_ge(ya_ready, g.n + 1)
                after(dve, yo_ready, g.n - 1)
                row = rows_in[:, bass.ds(g.n, 1), :].rearrange("p a d -> p (a d)")
                dve.scalar_tensor_tensor(out=yb[g.par][:], in0=bank_y[g.par][:, D:2 * D], scalar=row[:, WA + 1:WA + 2],
                                         in1=ya[g.par][:], op0=ALU.mult, op1=ALU.add).then_inc(yb_ready, 1)

            def tiles(g0, g1, g2, g3, g4, g5, g6):
                if g2:
                    place_weights(g2)
                if g0:
                    normal_row(g0)
                if g4:
                    rest_h(g4)
                if g2:
                    rest_x(g2)
                if g6:
                    both_experts(g6)

            dve.wait_ge(tab_ready, 2)
            pipeline(dve, TILES, 7, tiles, unroll=U, begin=load_experts)

        @block.tensor
        def _(pe):
            pe.wait_ge(pool_c, POOL_BLANK)
            pe.wait_ge(dve_c, DVE_GATE)

            def turn_adj(g, t):
                if t == 0:
                    pe.wait_ge(adj_in[g.par], 16 * (g.turn + 1))
                after(pe, adj_t_ready, T * g.n + t - 1)
                for r in range(T):
                    last = pe.transpose(bank_a[t % 2][:, r * P:(r + 1) * P], adj_s[g.par][:, r, t * P:(t + 1) * P], ident[:])
                last.then_inc(adj_t_made, 1)

            def turn_xn(g):
                pe.wait_ge(xn_ready, g.n + 1)
                after(pe, x2_t_ready, g.n - 1)
                for t in range(T):
                    last = pe.transpose(bank_x[:, t * P:(t + 1) * P], xn_s[g.par][:, t, :], ident[:])
                last.then_inc(xn_t_made, 1)

            def product(g):
                pe.wait_ge(sxn_ready, g.n + 1)
                pe.wait_ge(adj_t_ready, T * (g.n + 1))
                after(pe, z_ready, g.n)
                for t in range(T):
                    mm = pe.matmul(bank_z[:], sxn[g.par][:, t, :], adj_t[g.par][:, t, :], start=(t == 0), stop=(t == T - 1))
                mm.then_inc(z_made, 1)

            def own_part(g):
                pe.wait_ge(xn_t_ready, g.n + 1)
                after(pe, p_ready, g.n)
                for t in range(T):
                    mm = pe.matmul(bank_p[:, t * D:(t + 1) * D], xn_t[g.par][:, t * P:(t + 1) * P], w_sum[:],
                                   start=True, stop=True)
                mm.then_inc(p_made, 1)

            def neighbour_part(g):
                pe.wait_ge(z_ready, g.n + 1)
                after(pe, pre_ready, g.n)
                for t in range(T):
                    mm = pe.matmul(bank_g[:, t * D:(t + 1) * D], z_t[g.par][:, 0, t * P:(t + 1) * P], w_neigh_s[:],
                                   start=True, stop=True)
                mm.then_inc(g_made, 1)

            def turn_x2(g):
                pe.wait_ge(x2_ready, g.n + 1)
                pe.wait_ge(xn_t_ready, min(g.n + 2, B) if isinstance(g.n, int) else g.n + 2)
                for t in range(T):
                    last = pe.transpose(bank_x[:, t * P:(t + 1) * P], x2[g.par][:, t, :], ident[:])
                last.then_inc(x2_t_made, 1)

            def gate(g):
                after(pe, gap_ready, g.n)
                pe.matmul(logits_p, one_row[:], gate_bias[:].rearrange("p t e -> p (t e)"), start=True, stop=False,
                          skip_group_check=True)
                pe.wait_ge(x2_t_ready, g.n + 1)
                for t in range(T):
                    mm = pe.matmul(bank_l[:, t * E:(t + 1) * E], x2_t[g.par][:, t * P:(t + 1) * P], w_gate_s[:],
                                   start=False, stop=(t == T - 1), skip_group_check=True)
                mm.then_inc(logits_made, 1)

            def pair_cols(lo, hi):
                return bank_r[:, lo * NPAIR:hi * NPAIR]

            def count_before(g):
                pe.wait_ge(pick_ready, g.n + 1)
                for t in range(T):
                    mm = pe.matmul(pair_cols(t, t + 1), before[:], pick[g.par][:, t, :], start=False, stop=False,
                                   skip_group_check=True)
                    if t < T - 1:
                        pe.matmul(pair_cols(t + 1, T), ones_bf[:],
                                  pick[g.par][:, t, :].unsqueeze(1).broadcast_to([P, T - 1 - t, NPAIR]),
                                  start=False, stop=False, skip_group_check=True)
                mm.then_inc(rank_made, 1)

            def count_rest(g):
                pe.wait_ge(slot_ready, g.n + 1)
                for t in range(T):
                    mm = pe.matmul(pair_cols(t, t + 1), upto[:], pick[g.par][:, t, :], start=False, stop=False,
                                   skip_group_check=True)
                    if t > 0:
                        mm = pe.matmul(pair_cols(0, t), ones_bf[:],
                                       pick[g.par][:, t, :].unsqueeze(1).broadcast_to([P, t, NPAIR]),
                                       start=False, stop=False, skip_group_check=True)
                mm.then_inc(counted, 1)

            def graphs(g0, g1, g2, g3):
                if g0:
                    turn_adj(g0, 0)
                    turn_adj(g0, 1)
                if g1:
                    own_part(g1)
                    product(g1)
                if g3:
                    count_before(g3)
                if g0:
                    turn_adj(g0, 2)
                if g1:
                    neighbour_part(g1)
                if g2:
                    turn_x2(g2)
                if g0:
                    turn_adj(g0, 3)
                if g3:
                    count_rest(g3)
                if g2:
                    gate(g2)
                if g0:
                    turn_xn(g0)

            def between(i):
                if i == 0:
                    pe.wait_ge(pool_c, POOL_ALL)
                    pe.matmul(rank_p, p_row[:], pair_base[:].rearrange("p t q -> p (t q)"), start=True, stop=False,
                              skip_group_check=True)

            pipeline(pe, B, 4, graphs, between=between)
            pe.matmul(pair_cols(0, 1), zero_bf[:], pick[0][:, 0, :], start=False, stop=True,
                      skip_group_check=True).then_inc(count_made, 1)
            pe.wait_ge(tab_ready, 1)
            for c in range(3):
                mm = pe.matmul(bank_z[0:1, c * P:(c + 1) * P], tab_cols[:, c:c + 1], ident[:], start=True, stop=True)
            mm.then_inc(tab_t, 1)

            pe.wait_ge(tab_ready, 2)

            def turn_rows(g):
                pe.wait_ge(tn_ready, g.n + 1)
                after(pe, tl_ready, g.n - 1)
                pe.transpose(bank_t[g.par][:, 0:P], tn[g.par][:], ident[:]).then_inc(t_made, 1)

            def first_layer(g):
                pe.wait_ge(tl_ready, g.n + 1)
                pe.wait_ge(w_placed, g.n + 1)
                pe.wait_ge(b_placed, g.n + 1)
                after(pe, hl_ready, g.n - 1)
                for k in range(2):
                    for c in range(HC):
                        o = bank_h[g.par][:, (k * HC + c) * P:(k * HC + c + 1) * P]
                        lead, rest = (w_two[g.slot][:, k, i, c * P:(c + 1) * P] for i in (0, 1))
                        pe.matmul(o, b_two[g.slot][:, k, c * P:(c + 1) * P], ones_bf[:], start=True, stop=False)
                        pe.matmul(o, rest, th[g.par][:], start=False, stop=False)
                        pe.matmul(o, lead, tl[g.par][:], start=False, stop=False)
                        mm = pe.matmul(o, lead, th[g.par][:], start=False, stop=True)
                mm.then_inc(h_made, 1)

            def second_layer(g):
                pe.wait_ge(hl_ready, g.n + 1)
                after(pe, yb_ready, g.n - 1)
                for k in range(2):
                    o = bank_y[g.par][:, k * D:(k + 1) * D]
                    pe.matmul(o, ones_bf[:], b_two[g.slot][:, k, H:H + D], start=True, stop=False)
                    for c in range(HC):
                        w_lead, w_rest = (w_two[g.slot][:, k, i, c * D:(c + 1) * D] for i in (2, 3))
                        lead, rest = (v[g.par][:, (k * HC + c) * P:(k * HC + c + 1) * P] for v in (hh, hl))
                        pe.matmul(o, rest, w_lead, start=False, stop=False)
                        pe.matmul(o, lead, w_rest, start=False, stop=False)
                        mm = pe.matmul(o, lead, w_lead, start=False, stop=(c == HC - 1))
                mm.then_inc(y_made, 1)

            def tiles(g0, g1, g2, g3, g4, g5):
                if g1:
                    turn_rows(g1)
                if g3:
                    first_layer(g3)
                if g5:
                    second_layer(g5)

            pipeline(pe, TILES, 6, tiles, unroll=U)


_INS = ["x", "adj", "L0_gnn_gamma", "L0_gnn_beta", "L0_gnn_W_self", "L0_gnn_W_neigh", "L0_ffn_Wg", "L0_ffn_bg",
        "L0_ffn_bias", "L0_ffn_W1", "L0_ffn_b1", "L0_ffn_W2", "L0_ffn_b2"]


def kernel(**inputs):
    import numpy as _np
    import concourse.bacc as _bacc
    from concourse import mybir as _mybir
    from concourse.bass_utils import run_bass_kernel_spmd as _run

    nc = _bacc.Bacc("TRN2", target_bir_lowering=False, num_devices=1)
    arrays, args = {}, []
    for name in _INS:
        a = _np.ascontiguousarray(inputs[name])
        arrays[f"in_{name}_dram"] = a
        args.append(nc.dram_tensor(f"in_{name}_dram", a.shape, _mybir.dt.from_np(a.dtype), kind="ExternalInput").ap())
    shape = inputs["x"].shape
    args.append(nc.dram_tensor("out_dram", shape, _mybir.dt.float32, kind="ExternalOutput").ap())
    gnn_moe_kernel(nc, *args)
    r = _run(nc, [arrays], core_ids=[0])
    return r.results[0]["out_dram"]
```

```python
from contextlib import ExitStack

import concourse.bass as bass
from concourse import mybir

F32 = mybir.dt.float32
BF16 = mybir.dt.bfloat16
F16 = mybir.dt.float16
I32 = mybir.dt.int32
ALU = mybir.AluOpType
ACT = mybir.ActivationFunctionType
AX_X = mybir.AxisListType.X
RMAX = bass.bass_isa.ReduceOp.max

P = 128
EPS = 1e-5



def gnn_moe_kernel(nc, x, adj, gamma, beta, w_self, w_neigh, w_gate, b_gate, bias_gate, w1, b1, w2, b2, out):
    B, N, D = x.shape
    E, _, H = w1.shape
    T = N // P
    HC = H // P
    TOKENS = B * N
    PAIRS = [(a, b) for a in range(E) for b in range(a + 1, E)]
    NPAIR = len(PAIRS)
    REGION = TOKENS + P
    DUMMY = NPAIR * REGION
    FULL = TOKENS // P
    TILES = FULL + NPAIR
    ROW = D + 8
    SHIFT, RSTD, WA, TOKEN = D, D + 1, D + 2, D + 4
    BOUND = 40.0
    SKIPPED = 1 << 20
    TURNS = B // 2
    assert N == T * P == 512 and D == P and E == 8 and B % 2 == 0 and HC == 2

    sorted_rows = nc.dram_tensor("sorted_rows", (DUMMY + P, ROW), F32, kind="Internal").ap()
    b1_parts = nc.dram_tensor("b1_parts", (3, E * H), BF16, kind="Internal").ap()
    b2_parts = nc.dram_tensor("b2_parts", (3, E * D), BF16, kind="Internal").ap()
    x_v = x.rearrange("b (t p) d -> b p t d", p=P)
    adj_v = adj.rearrange("b (t p) j -> b p t j", p=P)
    out_rows = out.rearrange("b n d -> (b n) d")

    with ExitStack() as ctx:
        def sb(name, shape, dt=F32):
            return ctx.enter_context(nc.sbuf_tensor(name, shape, dt))

        def pair_of(name, shape, dt=F32):
            return [sb(f"{name}{i}", shape, dt) for i in range(2)]

        def bank(name):
            return ctx.enter_context(nc.psum_tensor(name, [P, 512], F32))

        def sem(name):
            return ctx.enter_context(nc.semaphore(name))

        def sem2(name):
            return [sem(f"{name}{i}") for i in range(2)]

        ident = sb("ident", [P, P])
        ones_bf = sb("ones_bf", [P, P], BF16)
        before = sb("before", [P, P], BF16)
        upto = sb("upto", [P, P], BF16)
        one_row = sb("one_row", [1, P])
        zero4 = sb("zero4", [P, T], I32)
        zero_i = sb("zero_i", [P, 1], I32)
        zero_bf = sb("zero_bf", [P, P], BF16)
        p_row = sb("p_row", [1, P])
        step4 = sb("step4", [P, T], I32)
        gamma_b = sb("gamma_b", [P, D])
        beta_b = sb("beta_b", [P, D])
        w_self_s = sb("w_self_s", [P, D])
        w_neigh_s = sb("w_neigh_s", [P, D])
        w_sum = sb("w_sum", [P, D])
        w_gate_s = sb("w_gate_s", [P, E])
        gate_row = sb("gate_row", [1, 2, E])
        gate_bias = sb("gate_bias", [1, T, E])
        rev = sb("rev", [P, E])
        codes = sb("codes", [P, NPAIR])
        pair_base = sb("pair_base", [1, T, NPAIR])
        pair_base_all = sb("pair_base_all", [P, NPAIR])
        pair_a = sb("pair_a", [P, NPAIR])
        pair_b = sb("pair_b", [P, NPAIR])
        tile_no = sb("tile_no", [P, 1])
        w1f = sb("w1f", [P, E, H])
        w2f = sb("w2f", [P, E, HC, D])
        w_all = sb("w_all", [P, E, 4, H], F16)
        NB1, NB2 = E * H // P, E * D // P
        b_all = sb("b_all", [P, E, H + D], BF16)
        b_cols = sb("b_cols", [P, NB1 + NB2])
        b_rest = sb("b_rest", [P, 2, NB1 + NB2])
        b_parts = sb("b_parts", [P, 3, NB1 + NB2], BF16)
        peak = sb("peak", [P, 4])
        peak2 = sb("peak2", [P, 2])
        peak_all = sb("peak_all", [P, 2])
        peak_c = sb("peak_c", [P, 2])
        expo = sb("expo", [P, 2], I32)
        scale_f = sb("scale_f", [P, 2])
        inv_f = sb("inv_f", [P, 2])
        scale12 = sb("scale12", [P, 1])
        inv12 = sb("inv12", [P, 1])
        blank_rows = sb("blank_rows", [P, ROW])

        rows_in = sb("rows_in", [P, TILES, ROW])
        shared = rows_in[:].rearrange("p a d -> p (a d)")
        used = [0]

        def view(dims):
            lo = used[0]
            used[0] += dims[0] * dims[1]
            assert used[0] <= TILES * ROW
            return shared[:, lo:used[0]].rearrange("p (a b) -> p a b", a=dims[0])

        adj_s = [view([T, N]) for _ in range(2)]
        adj_t = [view([T, N]) for _ in range(2)]
        unread = sb("unread", [P, T, N], BF16)
        x_s = [view([T, D]) for _ in range(2)]
        xr_s = [view([T, D]) for _ in range(2)]
        sxn = [view([T, D]) for _ in range(2)]
        z_t = [view([1, T * P]) for _ in range(2)]
        st = pair_of("st", [P, T, 6])
        mv = pair_of("mv", [P, T, 2])
        rs = pair_of("rs", [P, 4, T])
        rstd = pair_of("rstd", [P, T])
        u_rows = pair_of("u_rows", [P, T, D])
        xn_s = pair_of("xn_s", [P, T, D])
        xn_t = pair_of("xn_t", [P, T * P])
        deg = pair_of("deg", [P, 2, T])
        deg_c = pair_of("deg_c", [P, 2, T])
        deg_w = pair_of("deg_w", [P, 4, 2, T])
        s_deg = pair_of("s_deg", [P, 2, T])
        s_neg = pair_of("s_neg", [P, T])
        p_s = pair_of("p_s", [P, T * D])
        pre = pair_of("pre", [P, T * D])
        pre_c = pair_of("pre_c", [P, T * D])
        over = pair_of("over", [P, T, D])
        sp = pair_of("sp", [P, T, D])
        pay = pair_of("pay", [P, T, ROW])
        st2 = pair_of("st2", [P, T, 6])
        mv2 = pair_of("mv2", [P, T, 2])
        rs2 = pair_of("rs2", [P, 4, T])
        x2 = pair_of("x2", [P, T, D])
        x2_t = pair_of("x2_t", [P, T * P])
        lo8 = pair_of("lo8", [P, T, E])
        eq8 = pair_of("eq8", [P, T, E])
        ky8 = pair_of("ky8", [P, T, E])
        l28 = pair_of("l28", [P, T, E])
        m4 = pair_of("m4", [P, 6, T])
        e4 = pair_of("e4", [P, T])
        w4 = pair_of("w4", [P, 6, T])
        pick = pair_of("pick", [P, T, NPAIR], BF16)
        picked = pair_of("picked", [P, T, NPAIR])
        slot_f = pair_of("slot_f", [P, T])
        slot = pair_of("slot", [P, T], I32)
        tid = pair_of("tid", [P, T], I32)

        base_all = sb("base_all", [P, NPAIR])
        rest_no = sb("rest_no", [P, 1])
        any_pair = sb("any_pair", [P, 1])
        tab_cols = sb("tab_cols", [P, 3])
        cnt_i = sb("cnt_i", [P, 2, NPAIR], I32)
        n_full = sb("n_full", [P, NPAIR])
        ends = sb("ends", [P, NPAIR])
        starts = sb("starts", [P, NPAIR])
        inside = sb("inside", [P, 4, NPAIR])
        row_of = sb("row_of", [P, NPAIR])
        vals = sb("vals", [P, 5])
        tile_row = sb("tile_row", [P, 4])
        prod = sb("prod", [P, 5, NPAIR])
        ones_pair = sb("ones_pair", [P, NPAIR])
        rest_of = sb("rest_of", [P, NPAIR])
        rest_row = sb("rest_row", [P, NPAIR])
        table = sb("table", [1, P, 3], I32)
        pad_row = sb("pad_row", [1, NPAIR], I32)

        token = [sb(f"token{i}", [P, 1], I32) for i in range(4)]
        w_two = [sb(f"w_two{i}", [P, 2, 4, H], F16) for i in range(4)]
        b_two = [sb(f"b_two{i}", [P, 2, H + D], BF16) for i in range(4)]
        tn = pair_of("tn", [P, D])
        th = pair_of("th", [P, P], F16)
        tl = pair_of("tl", [P, P], F16)
        hh = pair_of("hh", [P, 2 * HC * P], F16)
        hl = pair_of("hl", [P, 2 * HC * P], F16)
        ya = pair_of("ya", [P, D])
        yb = pair_of("yb", [P, D])
        yo = [sb(f"yo{i}", [P, D]) for i in range(4)]

        bank_a = [bank("bank_a0"), bank("bank_a1")]
        bank_x = bank("bank_x")
        bank_z = bank("bank_z")
        bank_p = bank("bank_p")
        bank_g = bank("bank_g")
        bank_l = bank("bank_l")
        bank_r = bank("bank_r")
        logits_p = bank_l[:, 0:T * E]
        rank_p = bank_r[:, 0:T * NPAIR]
        bank_t, bank_h, bank_y = [bank_x, bank_z], bank_a, [bank_p, bank_g]

        consts_in, weights_in = sem("consts_in"), sem("weights_in")
        adj_in, x_in, xr_in = sem2("adj_in"), sem2("x_in"), sem2("xr_in")
        scattered = sem2("scattered")
        bias_out, bias_placed = sem("bias_out"), sem("bias_placed")
        pads_out = sem("pads_out")
        tile_loaded = [sem(f"tile_loaded{i}") for i in range(4)]
        stored = [sem(f"stored{i}") for i in range(4)]
        pool_c, dve_c, act_c, peak_ready = sem("pool_c"), sem("dve_c"), sem("act_c"), sem("peak_ready")
        var_ready, y_ready = sem("var_ready"), sem("y_ready")
        u_ready, ug_ready, xn_ready = sem("u_ready"), sem("ug_ready"), sem("xn_ready")
        xn_t_made, xn_t_ready = sem("xn_t_made"), sem("xn_t_ready")
        adj_t_made, adj_t_ready = sem("adj_t_made"), sem("adj_t_ready")
        deg_ready, degy_ready, sxn_ready = sem("deg_ready"), sem("degy_ready"), sem("sxn_ready")
        z_made, z_ready, p_made, p_ready = sem("z_made"), sem("z_ready"), sem("p_made"), sem("p_ready")
        g_made, pre_ready, ln_ready = sem("g_made"), sem("pre_ready"), sem("ln_ready")
        x1_ready, var2_ready, y2_ready, x2_ready = sem("x1_ready"), sem("var2_ready"), sem("y2_ready"), sem("x2_ready")
        x2_t_made, x2_t_ready = sem("x2_t_made"), sem("x2_t_ready")
        logits_made, gap_ready, e_ready = sem("logits_made"), sem("gap_ready"), sem("e_ready")
        pick_ready, rank_made, slot_ready = sem("pick_ready"), sem("rank_made"), sem("slot_ready")
        pay_ready, sdeg_ready, norm2_ready = sem("pay_ready"), sem("sdeg_ready"), sem("norm2_ready")
        over_added = sem("over_added")
        degc_ready, w_ready, counted = sem("degc_ready"), sem("w_ready"), sem("counted")
        stat_steps, norm_steps, degree_steps = sem("stat_steps"), sem("norm_steps"), sem("degree_steps")
        pre_steps, stat2_steps, norm2_steps = sem("pre_steps"), sem("stat2_steps"), sem("norm2_steps")
        choose_steps, place_steps, share_steps = sem("choose_steps"), sem("place_steps"), sem("share_steps")
        ln_var_ready, ln_deg_ready, exp_ready, ln_var2_ready = (
            sem("ln_var_ready"), sem("ln_deg_ready"), sem("exp_ready"), sem("ln_var2_ready"))
        token_steps, weight_steps = sem("token_steps"), sem("weight_steps")
        count_made, tab_steps, tab_ready, tab_turned = (
            sem("count_made"), sem("tab_steps"), sem("tab_ready"), sem("tab_turned"))
        w_placed, b_placed = sem("w_placed"), sem("b_placed")
        tn_ready, t_made, th_ready, tl_ready = sem("tn_ready"), sem("t_made"), sem("th_ready"), sem("tl_ready")
        h_made, hh_ready, hl_ready = sem("h_made"), sem("hh_ready"), sem("hl_ready")
        y_made, ya_ready, yb_ready, sum_ready, yo_ready = (
            sem("y_made"), sem("ya_ready"), sem("yb_ready"), sem("sum_ready"), sem("yo_ready"))

        class Item:

            def __init__(self, n, par, turn, slot):
                self.n, self.par, self.turn, self.slot = n, par, turn, slot

        def item(n, unroll=2):
            return Item(n, n % 2, n // unroll, n % unroll)

        def pipeline(eng, count, stages, step, unroll=2, between=None, begin=None):
            def at(i):
                return item(i, unroll) if 0 <= i < count else None

            peeled = -(-(stages - 1 + unroll) // unroll) * unroll
            for i in range(peeled):
                if begin and i % unroll == 0:
                    begin(i)
                step(*[at(i - j) for j in range(stages)])
                if between:
                    between(i)
            with eng.Fori(peeled // unroll, count // unroll) as turn:
                if begin:
                    begin(turn * unroll)
                for i in range(unroll):
                    step(*[Item(turn * unroll + (i - j), (i - j) % 2, turn + (i - j) // unroll, (i - j) % unroll)
                           for j in range(stages)])
            for i in range(count, count + stages - 1):
                if begin and i % unroll == 0:
                    begin(i)
                step(*[at(i - j) for j in range(stages)])
                if between:
                    between(i)

        def after(eng, signal, value):
            if not isinstance(value, int) or value > 0:
                eng.wait_ge(signal, value)

        def apart(eng, met, signal, value):
            if not isinstance(value, int):
                value = eng.to_reg(value)
            eng.wait_ge(*met)
            eng.wait_ge(signal, value)

        class Steps:

            def __init__(self, eng, own, n, per):
                self.eng, self.own, self.base, self.per, self.n = eng, own, n * per, per, 0

            def then(self, ins, met=None):
                self.n += 1
                assert self.n <= self.per
                ins.then_inc(self.own, 1)
                value = self.base + self.n
                yield
                if met:
                    apart(self.eng, met, self.own, value)
                else:
                    self.eng.wait_ge(self.own, value)

            def close(self):
                assert self.n == self.per, (self.n, self.per)

        def weave(*chains):
            chains = [c for c in chains if c]
            while chains:
                for c in list(chains):
                    if next(c, chains) is chains:
                        chains.remove(c)

        def each(ap, n):
            return ap.unsqueeze(2).broadcast_to([P, T, n])

        def per_tile(ap, n):
            return ap.unsqueeze(1).broadcast_to([P, T, n])

        U = 4
        POOL_BLANK, POOL_ALL = 6, 19
        DVE_GATE, DVE_PEAK, DVE_BIAS, DVE_ALL = 2, 4, 16, 18

        def expert_numbers(eng, i, stage):
            first, count = i - stage, U
            if isinstance(i, int):
                first, count = max(first, 0), max(min(i - stage + U, TILES) - max(first, 0), 0)
            if not count:
                return {}
            _, numbers = nc.values_load_multi_w_load_instructions(
                table[0:1, bass.ds(first, count), 1:3], engines=[eng.engine], min_val=0, max_val=E - 1,
                skip_runtime_bounds_check_because="the table was made with numbers of experts alone")
            slot = first % U if isinstance(i, int) else -stage % U
            return {(slot + k) % U: numbers[2 * k:2 * k + 2] for k in range(count)}

        block = ctx.enter_context(nc.Block())

        @block.sync
        def _(sp_e):
            def load_graph(g):
                after(sp_e, u_ready, g.n - 1)
                sp_e.dma_start(x_s[g.par][:], x_v[g.n]).then_inc(x_in[g.par], 16)
                after(sp_e, adj_t_made, T * (g.n - 1))
                after(sp_e, deg_ready, g.n - 1)
                sp_e.dma_start(adj_s[g.par][:], adj_v[g.n]).then_inc(adj_in[g.par], 16)

            def load_again(g):
                after(sp_e, x1_ready, g.n - 1)
                sp_e.dma_start(xr_s[g.par][:], x_v[g.n]).then_inc(xr_in[g.par], 16)

            def load(g0, g1):
                if g0:
                    load_graph(g0)
                if g1:
                    load_again(g1)

            def load_rest(i):
                if i == 0:
                    for dst, src in ((gamma_b[:], gamma.partition_broadcast(P)), (beta_b[:], beta.partition_broadcast(P)),
                                     (w_self_s[:], w_self), (w_neigh_s[:], w_neigh), (w_gate_s[:], w_gate),
                                     (gate_row[:, 0, :], b_gate.unsqueeze(0)),
                                     (gate_row[:, 1, :], bias_gate.unsqueeze(0))):
                        sp_e.dma_start(dst, src).then_inc(consts_in, 16)
                if i == 1:
                    b1_v = b1.rearrange("e h -> (e h)").rearrange("(p c) -> p c", p=P)
                    b2_v = b2.rearrange("e d -> (e d)").rearrange("(p c) -> p c", p=P)
                    for dst, src in ((w1f[:], w1.rearrange("e d h -> d e h")),
                                     (w2f[:], w2.rearrange("e (c h) d -> h e c d", h=P)),
                                     (b_cols[:, 0:NB1], b1_v), (b_cols[:, NB1:NB1 + NB2], b2_v)):
                        sp_e.dma_start(dst, src).then_inc(weights_in, 16)
                    sp_e.wait_ge(pool_c, POOL_BLANK)
                    sp_e.dma_start(sorted_rows[DUMMY:DUMMY + P, :], blank_rows[:]).then_inc(pads_out, 16)

            pipeline(sp_e, B, 2, load, between=load_rest)

            sp_e.wait_ge(pool_c, POOL_ALL)
            sp_e.wait_ge(dve_c, DVE_BIAS)
            sp_e.dma_start(b1_parts.rearrange("s (p c) -> p s c", p=P), b_parts[:, :, 0:NB1]).then_inc(bias_out, 16)
            sp_e.dma_start(b2_parts.rearrange("s (p c) -> p s c", p=P), b_parts[:, :, NB1:NB1 + NB2]).then_inc(bias_out, 16)
            sp_e.wait_ge(bias_out, 16 * 2)
            sp_e.dma_start(b_all[0:3, :, 0:H], b1_parts.rearrange("s (e h) -> s e h", e=E)).then_inc(bias_placed, 16)
            sp_e.dma_start(b_all[0:3, :, H:H + D], b2_parts.rearrange("s (e h) -> s e h", e=E)).then_inc(bias_placed, 16)

            sp_e.wait_ge(tab_ready, 2)
            for par in range(2):
                sp_e.wait_ge(scattered[par], 16 * T * TURNS)
            sp_e.wait_ge(pads_out, 16)

            def load_tile(g):
                row = sp_e.value_load(table[0:1, bass.ds(g.n, 1), 0], min_val=0, max_val=DUMMY)
                after(sp_e, tile_loaded[g.slot], 16 * g.turn)
                sp_e.wait_ge(tab_ready, 2)
                sp_e.dma_start(rows_in[:, bass.ds(g.n, 1), :].rearrange("p a d -> p (a d)"),
                               sorted_rows[bass.ds(row, P), :]).then_inc(tile_loaded[g.slot], 16)

            def pad(q):
                row = sp_e.value_load(pad_row[0:1, bass.ds(q, 1)], min_val=0, max_val=DUMMY)
                sp_e.dma_start(sorted_rows[bass.ds(row, P), :], blank_rows[:]).then_inc(pads_out, 16)

            for i in range(U):
                load_tile(item(i, U))
            with sp_e.Fori(1, FULL // U) as turn:
                for i in range(U):
                    load_tile(Item(turn * U + i, i % 2, turn, i))
            with sp_e.Fori(0, NPAIR) as q:
                pad(q)
            sp_e.wait_ge(pads_out, 16 * (NPAIR + 1))
            with sp_e.Fori(FULL // U, TILES // U) as turn:
                for i in range(U):
                    load_tile(Item(turn * U + i, i % 2, turn, i))
            for i in range(U):
                sp_e.wait_ge(stored[i], 16 * (TILES // U))

        @block.gpsimd
        def _(pool):
            count = [0]

            def made(ins, wait=False):
                count[0] += 1
                ins.then_inc(pool_c, 1)
                if wait:
                    pool.wait_ge(pool_c, count[0])

            made(pool.memset(ident[:], 0.0), True)
            made(pool.affine_select(out=ident[:], in_=ident[:], compare_op=ALU.not_equal, fill=1.0, base=0,
                                    pattern=[[-1, P]], channel_multiplier=1))
            made(pool.memset(one_row[:], 1.0))
            made(pool.memset(blank_rows[:], 0.0), True)
            made(pool.memset(blank_rows[:, TOKEN:TOKEN + 1].bitcast(I32), SKIPPED))
            made(pool.memset(zero4[:], 0))
            assert count[0] == POOL_BLANK

            def constants():
                made(pool.memset(step4[:], 2 * N))
                for par in range(2):
                    made(pool.memset(pay[par][:], 0.0))
                    made(pool.iota(tid[par][:], [[P, T]], base=par * N, channel_multiplier=1,
                                   allow_small_or_imprecise_dtypes=True))
                pool.wait_ge(pool_c, count[0])
                pool.memset(ones_pair[:], 1.0)
                pool.memset(zero_i[:], 0)
                pool.memset(zero_bf[:], 0.0)
                pool.memset(p_row[:], float(P))
                pool.memset(ones_bf[:], 1.0)
                made(pool.memset(b_all[:], 0.0))
                made(pool.memset(before[:], 1.0))
                made(pool.memset(upto[:], 1.0), True)
                made(pool.affine_select(out=before[:], in_=before[:], compare_op=ALU.is_gt, fill=0.0, base=0,
                                        pattern=[[1, P]], channel_multiplier=-1))
                made(pool.affine_select(out=upto[:], in_=upto[:], compare_op=ALU.is_ge, fill=0.0, base=0,
                                        pattern=[[-1, P]], channel_multiplier=1))
                for e in range(E):
                    pool.memset(rev[:, e:e + 1], float(2 ** (E - 1 - e)))
                for q, (a, b) in enumerate(PAIRS):
                    pool.memset(codes[:, q:q + 1], float(2 ** (E - 1 - a) + 2 ** (E - 1 - b)))
                    pool.memset(pair_a[:, q:q + 1], float(a))
                    pool.memset(pair_b[:, q:q + 1], float(b))
                made(pool.iota(pair_base[:], [[0, T], [REGION // P, NPAIR]], base=0, channel_multiplier=0,
                               allow_small_or_imprecise_dtypes=True))
                made(pool.iota(pair_base_all[:], [[REGION // P, NPAIR]], base=0, channel_multiplier=0,
                               allow_small_or_imprecise_dtypes=True))
                made(pool.iota(tile_no[:], [[0, 1]], base=0, channel_multiplier=1,
                               allow_small_or_imprecise_dtypes=True))
                assert count[0] == POOL_ALL, count

            def affine(g):
                pool.wait_ge(u_ready, g.n + 1)
                after(pool, xn_t_made, g.n - 1)
                after(pool, sxn_ready, g.n - 1)
                pool.tensor_tensor(xn_s[g.par][:], u_rows[g.par][:], per_tile(gamma_b[:], D),
                                   ALU.mult).then_inc(ug_ready, 1)
                pool.wait_ge(ug_ready, g.n + 1)
                pool.tensor_tensor(xn_s[g.par][:], xn_s[g.par][:], per_tile(beta_b[:], D),
                                   ALU.add).then_inc(xn_ready, 1)

            def add_over(g):
                pool.wait_ge(pre_ready, g.n + 1)
                pool.wait_ge(xr_in[g.par], 16 * (g.turn + 1))
                pool.tensor_tensor(xr_s[g.par][:], xr_s[g.par][:], over[g.par][:], ALU.add).then_inc(over_added, 1)

            def residual(g):
                pool.wait_ge(ln_ready, g.n + 1)
                pool.wait_ge(over_added, g.n + 1)
                after(pool, scattered[g.par], 16 * T * g.turn)
                pool.tensor_tensor(pay[g.par][:, :, 0:D], sp[g.par][:], xr_s[g.par][:], ALU.add).then_inc(x1_ready, 1)
                s = Steps(pool, token_steps, g.n, 2)
                yield from s.then(pool.tensor_tensor(pay[g.par][:, :, TOKEN].bitcast(I32), tid[g.par][:], zero4[:], ALU.add))
                yield from s.then(pool.tensor_tensor(tid[g.par][:], tid[g.par][:], step4[:], ALU.add))
                s.close()

            def weights(g):
                w = w4[g.par]
                s = Steps(pool, weight_steps, g.n, 4)
                pool.wait_ge(w_ready, g.n + 1)
                yield from s.then(pool.tensor_tensor(w[:, 2, :], w[:, 1, :], e4[g.par][:], ALU.mult))
                yield from s.then(pool.tensor_tensor(w[:, 3, :], w[:, 1, :], w[:, 2, :], ALU.subtract))
                yield from s.then(pool.tensor_tensor(w[:, 5, :], w[:, 3, :], w[:, 4, :], ALU.mult))
                yield from s.then(pool.tensor_tensor(pay[g.par][:, :, WA], w[:, 2, :], w[:, 5, :], ALU.add))
                pool.tensor_tensor(pay[g.par][:, :, WA + 1], w[:, 1, :], w[:, 5, :],
                                   ALU.subtract).then_inc(pay_ready, 1)
                s.close()

            def scatter(g):
                n = g.n + 1 if isinstance(g.n, int) else pool.to_reg(g.n + 1)
                pool.wait_ge(pool_c, POOL_ALL)
                pool.wait_ge(pay_ready, n)
                pool.wait_ge(slot_ready, n)
                for t in range(T):
                    pool.indirect_dma_start(
                        sorted_rows[:, :], bass.IndirectOffsetOnAxis(ap=slot[g.par][:, t:t + 1], axis=0),
                        pay[g.par][:, t, :], None).then_inc(scattered[g.par], 16)

            def graphs(g0, g1, g2, g3):
                if g2:
                    add_over(g2)
                    weave(residual(g2))
                if g0:
                    affine(g0)
                if g3:
                    weave(weights(g3))
                    scatter(g3)

            def between(i):
                if i == 1:
                    pool.wait_ge(dve_c, DVE_PEAK)
                    pool.partition_all_reduce(peak_all[:], peak2[:], P, RMAX).then_inc(peak_ready, 1)

            constants()
            pool.wait_ge(consts_in, 16 * 7)
            pipeline(pool, B, 4, graphs, between=between)

            def rows_of(g):
                return rows_in[:, bass.ds(g.n, 1), :].rearrange("p a d -> p (a d)")

            def sum_experts(g):
                after(pool, stored[g.slot], 16 * g.turn)
                pool.wait_ge(pool_c, POOL_ALL)
                pool.wait_ge(ya_ready, g.n + 1)
                pool.tensor_tensor(yo[g.slot][:], ya[g.par][:], yb[g.par][:], ALU.add).then_inc(sum_ready, 1)
                pool.tensor_tensor(token[g.slot][:], rows_of(g)[:, TOKEN:TOKEN + 1].bitcast(I32), zero_i[:],
                                   ALU.add).then_inc(yo_ready, 1)

            def store_rows(g):
                apart(pool, (pool_c, POOL_ALL), yo_ready, g.n + 1)
                pool.indirect_dma_start(
                    out_rows, bass.IndirectOffsetOnAxis(ap=token[g.slot][:], axis=0),
                    yo[g.slot][:], None, bounds_check=TOKENS - 1, oob_is_err=False).then_inc(stored[g.slot], 16)

            def tiles(g0, g1):
                if g1:
                    store_rows(g1)
                if g0:
                    sum_experts(g0)

            pipeline(pool, TILES, 2, tiles, unroll=U)

        @block.scalar
        def _(act):
            act.preload_act_table_set("natural_log_exp_and_others")

            def root(dst, src, n):
                act.activation(dst[1], src, ACT.Ln).then_inc(n[0], 1)
                act.wait_ge(n[0], n[1])
                return act.activation(dst[0], dst[1], ACT.Exp, scale=-0.5)

            def first_guess(g):
                act.wait_ge(var_ready, g.n + 1)
                r = rs[g.par]
                root((r[:, 1, :], r[:, 2, :]), r[:, 0, :], (ln_var_ready, g.n + 1)).then_inc(y_ready, 1)

            def sum_rows(g):
                act.wait_ge(adj_in[g.par], 16 * (g.turn + 1))
                after(act, sdeg_ready, g.n - 1)
                for t in range(T):
                    last = act.activation(unread[:, t, :], adj_s[g.par][:, t, :], ACT.Copy,
                                          accum_out=deg[g.par][:, 0, t:t + 1])
                last.then_inc(deg_ready, 1)

            def evacuate(g, t):
                act.wait_ge(adj_t_made, T * g.n + t + 1)
                if t == 0:
                    after(act, z_made, g.n - 1)
                act.activation(adj_t[g.par][:, t, :], bank_a[t % 2][:], ACT.Copy,
                               accum_out=deg[g.par][:, 1, t:t + 1]).then_inc(adj_t_ready, 1)

            def degree_guess(g):
                act.wait_ge(degc_ready, g.n + 1)
                d = deg_w[g.par]
                root((d[:, 0], d[:, 1]), deg_c[g.par][:], (ln_deg_ready, g.n + 1)).then_inc(degy_ready, 1)

            def xn_out(g):
                act.wait_ge(xn_t_made, g.n + 1)
                after(act, p_made, g.n - 1)
                act.activation(xn_t[g.par][:], bank_x[:], ACT.Copy).then_inc(xn_t_ready, 1)

            def scale_xn(g):
                act.wait_ge(sdeg_ready, g.n + 1)
                act.wait_ge(xn_ready, g.n + 1)
                after(act, z_made, g.n - 1)
                for t in range(T):
                    last = act.activation(sxn[g.par][:, t, :], xn_s[g.par][:, t, :], ACT.Copy,
                                          scale=s_deg[g.par][:, 0, t:t + 1])
                last.then_inc(sxn_ready, 1)

            def p_out(g):
                act.wait_ge(p_made, g.n + 1)
                after(act, pre_ready, g.n - 1)
                act.activation(p_s[g.par][:], bank_p[:], ACT.Copy).then_inc(p_ready, 1)

            def softplus(g):
                act.wait_ge(pre_ready, g.n + 1)
                after(act, x1_ready, g.n - 1)
                act.activation(pre_c[g.par][:], pre_c[g.par][:], ACT.Exp).then_inc(exp_ready, 1)
                act.wait_ge(exp_ready, g.n + 1)
                act.activation(sp[g.par][:].rearrange("p t d -> p (t d)"), pre_c[g.par][:], ACT.Ln, bias=1.0).then_inc(ln_ready, 1)

            def second_guess(g):
                act.wait_ge(var2_ready, g.n + 1)
                r = rs2[g.par]
                root((r[:, 1, :], r[:, 2, :]), r[:, 0, :], (ln_var2_ready, g.n + 1)).then_inc(y2_ready, 1)

            def second_normalise(g):
                act.wait_ge(norm2_ready, g.n + 1)
                after(act, x2_t_made, g.n - 1)
                for t in range(T):
                    last = act.activation(x2[g.par][:, t, :], pay[g.par][:, t, 0:D], ACT.Identity,
                                          bias=pay[g.par][:, t, SHIFT:SHIFT + 1], scale=pay[g.par][:, t, RSTD:RSTD + 1])
                last.then_inc(x2_ready, 1)

            def x2_out(g):
                act.wait_ge(x2_t_made, g.n + 1)
                act.activation(x2_t[g.par][:], bank_x[:], ACT.Copy).then_inc(x2_t_ready, 1)

            def gate_exp(g):
                act.wait_ge(gap_ready, g.n + 1)
                after(act, pay_ready, g.n - 1)
                act.activation(e4[g.par][:], m4[g.par][:, 4, :], ACT.Exp).then_inc(e_ready, 1)

            def graphs(g0, g1, g2, g3, g4):
                if g1:
                    evacuate(g1, 2)
                    evacuate(g1, 3)
                if g0:
                    sum_rows(g0)
                if g1:
                    degree_guess(g1)
                if g4:
                    gate_exp(g4)
                if g0:
                    evacuate(g0, 0)
                if g3:
                    second_guess(g3)
                if g2:
                    p_out(g2)
                if g0:
                    first_guess(g0)
                if g1:
                    xn_out(g1)
                if g3:
                    second_normalise(g3)
                if g0:
                    evacuate(g0, 1)
                if g3:
                    x2_out(g3)
                if g1:
                    scale_xn(g1)
                if g2:
                    softplus(g2)

            def between(i):
                if i == B:
                    act.wait_ge(weights_in, 16 * 4)
                    act.wait_ge(dve_c, DVE_BIAS)
                    act.activation(w_all[:, :, 0, :], w1f[:], ACT.Copy,
                                   scale=scale_f[:, 0:1]).then_inc(act_c, 1)
                    act.activation(w_all[:, :, 2, :], w2f[:].rearrange("p e c d -> p e (c d)"), ACT.Copy,
                                   scale=scale_f[:, 1:2]).then_inc(act_c, 1)

            pipeline(act, B, 5, graphs, between=between)

            def normal_row(g):
                act.wait_ge(dve_c, DVE_ALL)
                act.wait_ge(tile_loaded[g.slot], 16 * (g.turn + 1))
                after(act, t_made, g.n - 1)
                row = rows_in[:, bass.ds(g.n, 1), :].rearrange("p a d -> p (a d)")
                act.activation(tn[g.par][:], row[:, 0:D], ACT.Identity, bias=row[:, SHIFT:SHIFT + 1],
                               scale=row[:, RSTD:RSTD + 1]).then_inc(tn_ready, 1)

            def lead_x(g):
                act.wait_ge(t_made, g.n + 1)
                act.activation(th[g.par][:], bank_t[g.par][:, 0:P], ACT.Copy).then_inc(th_ready, 1)

            def lead_h(g):
                act.wait_ge(h_made, g.n + 1)
                after(act, y_made, g.n - 1)
                act.activation(hh[g.par][:], bank_h[g.par][:], ACT.Relu).then_inc(hh_ready, 1)

            experts = {}

            def load_experts(n):
                experts.update(expert_numbers(act, n, 1))

            def place_biases(g):
                act.wait_ge(dve_c, DVE_ALL)
                after(act, y_made, g.n - (U - 1))
                act.activation(b_two[g.slot][:, 1], b_all[:, bass.ds(experts[g.slot][1], 1), :].rearrange(
                    "p e h -> p (e h)"), ACT.Copy).then_inc(b_placed, 1)

            def second_expert(g):
                act.wait_ge(dve_c, DVE_ALL)
                act.wait_ge(y_made, g.n + 1)
                after(act, sum_ready, g.n - 1)
                row = rows_in[:, bass.ds(g.n, 1), :].rearrange("p a d -> p (a d)")
                act.activation(yb[g.par][:], bank_y[g.par][:, D:2 * D], ACT.Copy,
                               scale=row[:, WA + 1:WA + 2]).then_inc(yb_ready, 1)

            def tiles(g0, g1, g2, g3, g4, g5):
                if g5:
                    second_expert(g5)
                if g3:
                    lead_h(g3)
                if g1:
                    place_biases(g1)
                if g0:
                    normal_row(g0)
                if g1:
                    lead_x(g1)

            act.wait_ge(tab_ready, 2)
            act.wait_ge(tab_ready, 2)
            act.wait_ge(bias_placed, 16 * 2)
            pipeline(act, TILES, 6, tiles, unroll=U, begin=load_experts)

        @block.vector
        def _(dve):
            count = [0]

            def made(ins, wait=True):
                count[0] += 1
                ins.then_inc(dve_c, 1)
                if wait:
                    dve.wait_ge(dve_c, count[0])

            def newton(s, r, arg, y, t1, t2, dst):
                yield from s.then(dve.scalar_tensor_tensor(out=t1, in0=y, scalar=-0.5, in1=arg, op0=ALU.mult, op1=ALU.mult))
                yield from s.then(dve.tensor_tensor(t2, t1, y, ALU.mult))
                yield from s.then(dve.scalar_tensor_tensor(out=dst, in0=t2, scalar=1.5, in1=y, op0=ALU.add, op1=ALU.mult))

            def statistics(g):
                dve.wait_ge(x_in[g.par], 16 * (g.turn + 1))
                s = Steps(dve, stat_steps, g.n, 2)
                for t in range(T):
                    last = dve.bn_stats(st[g.par][:, t, :], x_s[g.par][:, t, :])
                    if t < T - 1:
                        yield
                yield from s.then(last, met=(pool_c, 1))
                for t in range(T):
                    last = dve.bn_aggr(mv[g.par][:, t, :], st[g.par][:, t, :])
                yield from s.then(last)
                s.close()
                dve.tensor_scalar(rs[g.par][:, 0, :], mv[g.par][:, :, 1], 1.0 + EPS, EPS * EPS,
                                  ALU.mult, ALU.add).then_inc(var_ready, 1)

            def normalise(g):
                dve.wait_ge(y_ready, g.n + 1)
                r = rs[g.par]
                s = Steps(dve, norm_steps, g.n, 3)
                yield from newton(s, r, r[:, 0, :], r[:, 1, :], r[:, 2, :], r[:, 3, :], rstd[g.par][:])
                s.close()
                after(dve, ug_ready, g.n - 1)
                for t in range(T):
                    last = dve.tensor_scalar(u_rows[g.par][:, t, :], x_s[g.par][:, t, :], mv[g.par][:, t, 0:1],
                                             rstd[g.par][:, t:t + 1], ALU.subtract, ALU.mult)
                    if t < T - 1:
                        yield
                last.then_inc(u_ready, 1)

            def degrees(g):
                dve.wait_ge(deg_ready, g.n + 1)
                dve.wait_ge(adj_t_ready, T * (g.n + 1))
                dve.tensor_scalar(deg_c[g.par][:], deg[g.par][:], 1e-18, None, ALU.max).then_inc(degc_ready, 1)

            def scale_rows(g):
                dve.wait_ge(degy_ready, g.n + 1)
                after(dve, sxn_ready, g.n - 1)
                d = deg_w[g.par]
                s = Steps(dve, degree_steps, g.n, 5)
                yield from newton(s, None, deg_c[g.par][:], d[:, 0], d[:, 1], d[:, 2], d[:, 3])
                yield from s.then(dve.tensor_scalar(d[:, 1], deg[g.par][:], 0.0, None, ALU.not_equal))
                yield from s.then(dve.tensor_tensor(s_deg[g.par][:], d[:, 3], d[:, 1], ALU.mult))
                s.close()
                dve.tensor_scalar(s_neg[g.par][:], s_deg[g.par][:, 1, :], -1.0, None, ALU.mult).then_inc(sdeg_ready, 1)

            def z_out(g):
                dve.wait_ge(z_made, g.n + 1)
                after(dve, g_made, g.n - 1)
                dve.tensor_copy(z_t[g.par][:, 0, :], bank_z[:]).then_inc(z_ready, 1)

            def combine(g):
                dve.wait_ge(sdeg_ready, g.n + 1)
                dve.wait_ge(p_ready, g.n + 1)
                dve.wait_ge(g_made, g.n + 1)
                s = Steps(dve, pre_steps, g.n, 1)
                for t in range(T):
                    c = slice(t * D, (t + 1) * D)
                    last = dve.scalar_tensor_tensor(out=pre[g.par][:, c], in0=bank_g[:, c], scalar=s_neg[g.par][:, t:t + 1],
                                                    in1=p_s[g.par][:, c], op0=ALU.mult, op1=ALU.add)
                yield from s.then(last)
                s.close()
                after(dve, ln_ready, g.n - 1)
                after(dve, over_added, g.n - 1)
                dve.tensor_scalar(pre_c[g.par][:], pre[g.par][:], BOUND, None, ALU.min)
                dve.tensor_scalar(over[g.par][:].rearrange("p t d -> p (t d)"), pre[g.par][:], BOUND, 0.0,
                                  ALU.subtract, ALU.max).then_inc(pre_ready, 1)

            def second_norm(g):
                dve.wait_ge(x1_ready, g.n + 1)
                s = Steps(dve, stat2_steps, g.n, 2)
                for t in range(T):
                    last = dve.bn_stats(st2[g.par][:, t, :], pay[g.par][:, t, 0:D])
                    if t < T - 1:
                        yield
                yield from s.then(last, met=(pool_c, 1))
                for t in range(T):
                    last = dve.bn_aggr(mv2[g.par][:, t, :], st2[g.par][:, t, :])
                yield from s.then(last)
                s.close()
                dve.tensor_scalar(rs2[g.par][:, 0, :], mv2[g.par][:, :, 1], EPS, None, ALU.add).then_inc(var2_ready, 1)

            def second_root(g):
                r = rs2[g.par]
                dve.wait_ge(y2_ready, g.n + 1)
                s = Steps(dve, norm2_steps, g.n, 3)
                yield from newton(s, r, r[:, 0, :], r[:, 1, :], r[:, 2, :], r[:, 3, :], pay[g.par][:, :, RSTD])
                s.close()
                dve.scalar_tensor_tensor(out=pay[g.par][:, :, SHIFT], in0=mv2[g.par][:, :, 0], scalar=-1.0,
                                         in1=pay[g.par][:, :, RSTD], op0=ALU.mult, op1=ALU.mult).then_inc(norm2_ready, 1)

            def choose(g):
                i = g.par
                lo, eq, ky, l2, m = lo8[i][:], eq8[i][:], ky8[i][:], l28[i][:], m4[i]
                dve.wait_ge(logits_made, g.n + 1)
                after(dve, pay_ready, g.n - 1)
                after(dve, counted, g.n - 1)
                s = Steps(dve, choose_steps, g.n, 12)
                yield from s.then(dve.tensor_copy(lo, logits_p))
                yield from s.then(dve.tensor_reduce(m[:, 0, :], lo, AX_X, ALU.max))
                yield from s.then(dve.tensor_tensor(eq, lo, each(m[:, 0, :], E), ALU.is_equal))
                yield from s.then(dve.tensor_tensor(ky, eq, per_tile(rev[:], E), ALU.mult))
                yield from s.then(dve.tensor_reduce(m[:, 1, :], ky, AX_X, ALU.max))
                yield from s.then(dve.tensor_tensor(eq, per_tile(rev[:], E), each(m[:, 1, :], E), ALU.is_equal))
                yield from s.then(dve.scalar_tensor_tensor(out=l2, in0=eq, scalar=-3.0e38, in1=lo, op0=ALU.mult, op1=ALU.add))
                yield from s.then(dve.tensor_reduce(m[:, 2, :], l2, AX_X, ALU.max))
                dve.tensor_tensor(m[:, 4, :], m[:, 2, :], m[:, 0, :], ALU.subtract).then_inc(gap_ready, 1)
                yield from s.then(dve.tensor_tensor(eq, l2, each(m[:, 2, :], E), ALU.is_equal))
                yield from s.then(dve.tensor_tensor(ky, eq, per_tile(rev[:], E), ALU.mult))
                yield from s.then(dve.tensor_reduce(m[:, 3, :], ky, AX_X, ALU.max))
                dve.tensor_tensor(w4[i][:, 4, :], m[:, 1, :], m[:, 3, :], ALU.is_gt)
                yield from s.then(dve.tensor_tensor(m[:, 5, :], m[:, 1, :], m[:, 3, :], ALU.add))
                s.close()
                dve.tensor_tensor(pick[i][:], per_tile(codes[:], NPAIR), each(m[:, 5, :], NPAIR),
                                  ALU.is_equal).then_inc(pick_ready, 1)

            def share(g):
                w = w4[g.par]
                dve.wait_ge(e_ready, g.n + 1)
                s = Steps(dve, share_steps, g.n, 2)
                yield from s.then(dve.tensor_scalar(w[:, 0, :], e4[g.par][:], 1.0, None, ALU.add))
                yield from s.then(dve.reciprocal(w[:, 5, :], w[:, 0, :]))
                s.close()
                dve.tensor_scalar(w[:, 1, :], w[:, 5, :], inv12[:], None, ALU.mult).then_inc(w_ready, 1)

            def place(g):
                i = g.par
                dve.wait_ge(rank_made, g.n + 1)
                after(dve, scattered[i], 16 * T * g.turn)
                s = Steps(dve, place_steps, g.n, 2)
                yield from s.then(dve.tensor_tensor(picked[i][:], rank_p, pick[i][:], ALU.mult))
                yield from s.then(dve.tensor_reduce(slot_f[i][:], picked[i][:], AX_X, ALU.add))
                s.close()
                dve.tensor_copy(slot[i][:], slot_f[i][:]).then_inc(slot_ready, 1)

            def graphs(g0, g1, g2, g3, g4):
                if g1:
                    degrees(g1)
                weave(g3 and second_norm(g3), g0 and statistics(g0))
                weave(g4 and place(g4), g4 and share(g4))
                weave(g3 and second_root(g3), g1 and scale_rows(g1))
                if g2:
                    z_out(g2)
                    weave(combine(g2))
                weave(g3 and choose(g3), g0 and normalise(g0))

            def between(i):
                if i == 0:
                    dve.wait_ge(consts_in, 16 * 7)
                    made(dve.tensor_tensor(w_sum[:], w_self_s[:], w_neigh_s[:], ALU.add))
                    made(dve.tensor_tensor(gate_bias[:], gate_row[:, 0, :].unsqueeze(1).broadcast_to([1, T, E]),
                                           gate_row[:, 1, :].unsqueeze(1).broadcast_to([1, T, E]), ALU.add))
                    assert count[0] == DVE_GATE
                if i == 1:
                    dve.wait_ge(weights_in, 16 * 4)
                    dve.tensor_reduce(peak[:, 1:2], b_cols[:, 0:NB1], AX_X, ALU.max, apply_absolute_value=True)
                    dve.tensor_reduce(peak2[:, 1:2], w2f[:].rearrange("p e c d -> p (e c d)"), AX_X, ALU.max,
                                      apply_absolute_value=True)
                    made(dve.tensor_reduce(peak[:, 0:1], w1f[:].rearrange("p e h -> p (e h)"), AX_X, ALU.max,
                                           apply_absolute_value=True))
                    made(dve.tensor_tensor(peak2[:, 0:1], peak[:, 0:1], peak[:, 1:2], ALU.max))
                    assert count[0] == DVE_PEAK
                if i == 2:
                    dve.wait_ge(peak_ready, 1)
                    made(dve.tensor_scalar(peak_c[:], peak_all[:], 1e-9, None, ALU.max))
                    made(dve.tensor_scalar(expo[:], peak_c[:].bitcast(I32), 0x7F800000, None, ALU.bitwise_and))
                    made(dve.tensor_scalar(scale_f[:].bitcast(I32), expo[:], -1.0, float(261 << 23), ALU.mult, ALU.add))
                    made(dve.tensor_scalar(inv_f[:].bitcast(I32), expo[:], float(7 << 23), None, ALU.subtract))
                    made(dve.tensor_tensor(scale12[:], scale_f[:, 0:1], scale_f[:, 1:2], ALU.mult))
                    made(dve.tensor_tensor(inv12[:], inv_f[:, 0:1], inv_f[:, 1:2], ALU.mult))
                    dve.tensor_scalar(b_rest[:, 0, 0:NB1], b_cols[:, 0:NB1], scale_f[:, 0:1], None, ALU.mult)
                    made(dve.tensor_scalar(b_rest[:, 0, NB1:NB1 + NB2], b_cols[:, NB1:NB1 + NB2], scale12[:], None, ALU.mult))
                    made(dve.tensor_copy(b_parts[:, 0, :], b_rest[:, 0, :]))
                    made(dve.tensor_tensor(b_rest[:, 1, :], b_rest[:, 0, :], b_parts[:, 0, :], ALU.subtract))
                    made(dve.tensor_copy(b_parts[:, 1, :], b_rest[:, 1, :]))
                    made(dve.tensor_tensor(b_rest[:, 0, :], b_rest[:, 1, :], b_parts[:, 1, :], ALU.subtract))
                    made(dve.tensor_copy(b_parts[:, 2, :], b_rest[:, 0, :]))
                    assert count[0] == DVE_BIAS, count
                if i == B + 2:
                    dve.wait_ge(act_c, 2)
                    made(dve.scalar_tensor_tensor(out=w_all[:, :, 1, :], in0=w1f[:],
                                                  scalar=scale_f[:, 0:1], in1=w_all[:, :, 0, :], op0=ALU.mult, op1=ALU.subtract), False)
                    made(dve.scalar_tensor_tensor(out=w_all[:, :, 3, :], in0=w2f[:].rearrange("p e c d -> p e (c d)"),
                                                  scalar=scale_f[:, 1:2], in1=w_all[:, :, 2, :],
                                                  op0=ALU.mult, op1=ALU.subtract), False)
                    assert count[0] == DVE_ALL

            pipeline(dve, B, 5, graphs, between=between)

            tab = [0]

            def group(*instructions):
                for ins in instructions:
                    ins.then_inc(tab_steps, 1)
                tab[0] += len(instructions)
                dve.wait_ge(tab_steps, tab[0])

            group(dve.tensor_scalar(base_all[:], pair_base_all[:], float(P), None, ALU.mult),
                  dve.tensor_scalar(rest_no[:], tile_no[:], -float(FULL), float(REGION // P), ALU.add, ALU.mult),
                  dve.tensor_scalar(tile_row[:, 0:1], tile_no[:], float(P), None, ALU.mult))
            group(dve.tensor_scalar(rest_of[:], pair_base_all[:], rest_no[:], None, ALU.is_equal))
            dve.wait_ge(count_made, 1)
            group(dve.tensor_copy(pad_row[:], rank_p[0:1, 0:NPAIR]),
                  dve.tensor_tensor(cnt_i[:, 0, :], rank_p[:, 0:NPAIR], base_all[:], ALU.subtract))
            group(dve.tensor_scalar(cnt_i[:, 1, :], cnt_i[:, 0, :], 7, None, ALU.logical_shift_right))
            group(dve.tensor_copy(n_full[:], cnt_i[:, 1, :]))
            group(dve.tensor_tensor_scan(ends[:], ones_pair[:], n_full[:], 0.0, ALU.mult, ALU.add),
                  dve.scalar_tensor_tensor(out=rest_row[:], in0=n_full[:], scalar=float(P), in1=base_all[:],
                                           op0=ALU.mult, op1=ALU.add))
            group(dve.tensor_tensor(starts[:], ends[:], n_full[:], ALU.subtract),
                  dve.tensor_scalar(inside[:, 1, :], ends[:], tile_no[:], None, ALU.is_gt),
                  dve.tensor_tensor(prod[:, 1, :], rest_of[:], rest_row[:], ALU.mult))
            group(dve.tensor_scalar(inside[:, 0, :], starts[:], tile_no[:], None, ALU.is_le),
                  dve.scalar_tensor_tensor(out=row_of[:], in0=starts[:], scalar=-float(P), in1=base_all[:],
                                           op0=ALU.mult, op1=ALU.add))
            group(dve.tensor_tensor(inside[:, 2, :], inside[:, 0, :], inside[:, 1, :], ALU.mult))
            group(dve.tensor_tensor(inside[:, 3, :], inside[:, 2, :], rest_of[:], ALU.add),
                  dve.tensor_tensor(prod[:, 0, :], inside[:, 2, :], row_of[:], ALU.mult),
                  dve.tensor_copy(prod[:, 4, :], inside[:, 2, :]))
            group(dve.tensor_tensor(prod[:, 2, :], inside[:, 3, :], pair_a[:], ALU.mult),
                  dve.tensor_tensor(prod[:, 3, :], inside[:, 3, :], pair_b[:], ALU.mult),
                  dve.tensor_reduce(any_pair[:], inside[:, 3, :], AX_X, ALU.add))
            group(dve.tensor_reduce(vals[:], prod[:], AX_X, ALU.add),
                  dve.tensor_scalar(tile_row[:, 2:3], any_pair[:], -float(DUMMY), float(DUMMY), ALU.mult, ALU.add))
            group(dve.tensor_tensor(tile_row[:, 1:2], tile_row[:, 0:1], vals[:, 4:5], ALU.mult))
            group(dve.scalar_tensor_tensor(out=tile_row[:, 3:4], in0=tile_row[:, 1:2], scalar=vals[:, 0:1],
                                           in1=tile_row[:, 2:3], op0=ALU.add, op1=ALU.add))
            group(dve.tensor_tensor(vals[:, 1:2], tile_row[:, 3:4], vals[:, 1:2], ALU.add))
            dve.tensor_copy(tab_cols[:], vals[:, 1:4]).then_inc(tab_ready, 1)
            dve.wait_ge(tab_turned, 1)
            dve.tensor_copy(table[:].rearrange("p n c -> p c n"), bank_z[0:1, 0:3 * P].rearrange("p (c n) -> p c n", c=3)).then_inc(tab_ready, 1)

            experts = {}

            def load_experts(n):
                experts.update(expert_numbers(dve, n, 0))

            def place_weights(g):
                after(dve, y_made, g.n - (U - 1))
                for k, e in enumerate(experts[g.slot]):
                    dve.tensor_copy(w_two[g.slot][:, k].rearrange("p i h -> p (i h)"),
                                    w_all[:, bass.ds(e, 1), :, :].rearrange("p e i h -> p (e i h)"))
                dve.tensor_copy(b_two[g.slot][:, 0], b_all[:, bass.ds(experts[g.slot][0], 1), :].rearrange(
                    "p e h -> p (e h)")).then_inc(w_placed, 1)

            def rest_x(g):
                dve.wait_ge(th_ready, g.n + 1)
                dve.tensor_tensor(tl[g.par][:], bank_t[g.par][:, 0:P], th[g.par][:], ALU.subtract).then_inc(tl_ready, 1)

            def rest_h(g):
                dve.wait_ge(hh_ready, g.n + 1)
                dve.scalar_tensor_tensor(out=hl[g.par][:], in0=bank_h[g.par][:], scalar=0.0, in1=hh[g.par][:],
                                         op0=ALU.max, op1=ALU.subtract).then_inc(hl_ready, 1)

            def first_expert(g):
                dve.wait_ge(yb_ready, g.n + 1)
                after(dve, sum_ready, g.n - 1)
                row = rows_in[:, bass.ds(g.n, 1), :].rearrange("p a d -> p (a d)")
                dve.scalar_tensor_tensor(out=ya[g.par][:], in0=bank_y[g.par][:, 0:D], scalar=row[:, WA:WA + 1],
                                         in1=row[:, 0:D], op0=ALU.mult, op1=ALU.add).then_inc(ya_ready, 1)

            def tiles(g0, g1, g2, g3, g4):
                if g1:
                    rest_x(g1)
                if g4:
                    first_expert(g4)
                if g0:
                    place_weights(g0)
                if g2:
                    rest_h(g2)

            dve.wait_ge(tab_ready, 2)
            dve.wait_ge(bias_placed, 16 * 2)
            pipeline(dve, TILES, 5, tiles, unroll=U, begin=load_experts)

        @block.tensor
        def _(pe):
            pe.wait_ge(pool_c, POOL_BLANK)

            def turn_adj(g, t):
                if t == 0:
                    pe.wait_ge(adj_in[g.par], 16 * (g.turn + 1))
                after(pe, adj_t_ready, T * g.n + t - 1)
                for r in range(T):
                    last = pe.transpose(bank_a[t % 2][:, r * P:(r + 1) * P], adj_s[g.par][:, r, t * P:(t + 1) * P], ident[:])
                last.then_inc(adj_t_made, 1)

            def turn_xn(g):
                pe.wait_ge(xn_ready, g.n + 1)
                after(pe, xn_t_ready, g.n)
                after(pe, x2_t_ready, g.n - 2)
                for t in range(T):
                    last = pe.transpose(bank_x[:, t * P:(t + 1) * P], xn_s[g.par][:, t, :], ident[:])
                last.then_inc(xn_t_made, 1)

            def product(g):
                pe.wait_ge(sxn_ready, g.n + 1)
                pe.wait_ge(adj_t_ready, T * (g.n + 1))
                after(pe, z_ready, g.n)
                for t in range(T):
                    last_mm = pe.matmul(bank_z[:], sxn[g.par][:, t, :], adj_t[g.par][:, t, :], start=(t == 0), stop=(t == T - 1))
                last_mm.then_inc(z_made, 1)

            def own_part(g):
                pe.wait_ge(xn_t_ready, g.n + 1)
                after(pe, p_ready, g.n)
                for t in range(T):
                    last_mm = pe.matmul(bank_p[:, t * D:(t + 1) * D], xn_t[g.par][:, t * P:(t + 1) * P], w_sum[:],
                                   start=True, stop=True)
                last_mm.then_inc(p_made, 1)

            def neighbour_part(g):
                pe.wait_ge(z_ready, g.n + 1)
                after(pe, pre_ready, g.n)
                for t in range(T):
                    last_mm = pe.matmul(bank_g[:, t * D:(t + 1) * D], z_t[g.par][:, 0, t * P:(t + 1) * P], w_neigh_s[:],
                                   start=True, stop=True)
                last_mm.then_inc(g_made, 1)

            def turn_x2(g):
                pe.wait_ge(x2_ready, g.n + 1)
                pe.wait_ge(xn_t_ready, min(g.n + 3, B) if isinstance(g.n, int) else g.n + 3)
                for t in range(T):
                    last = pe.transpose(bank_x[:, t * P:(t + 1) * P], x2[g.par][:, t, :], ident[:])
                last.then_inc(x2_t_made, 1)

            def gate(g):
                after(pe, gap_ready, g.n)
                pe.matmul(logits_p, one_row[:], gate_bias[:].rearrange("p t e -> p (t e)"), start=True, stop=False,
                          skip_group_check=True)
                pe.wait_ge(x2_t_ready, g.n + 1)
                for t in range(T):
                    last_mm = pe.matmul(bank_l[:, t * E:(t + 1) * E], x2_t[g.par][:, t * P:(t + 1) * P], w_gate_s[:],
                                   start=False, stop=(t == T - 1), skip_group_check=True)
                last_mm.then_inc(logits_made, 1)

            def pair_cols(lo, hi):
                return bank_r[:, lo * NPAIR:hi * NPAIR]

            def count_before(g):
                pe.wait_ge(pick_ready, g.n + 1)
                for t in range(T):
                    last_mm = pe.matmul(pair_cols(t, t + 1), before[:], pick[g.par][:, t, :], start=False, stop=False,
                                   skip_group_check=True)
                    if t < T - 1:
                        pe.matmul(pair_cols(t + 1, T), ones_bf[:],
                                  pick[g.par][:, t, :].unsqueeze(1).broadcast_to([P, T - 1 - t, NPAIR]),
                                  start=False, stop=False, skip_group_check=True)
                last_mm.then_inc(rank_made, 1)

            def count_rest(g):
                pe.wait_ge(slot_ready, g.n + 1)
                for t in range(T):
                    last_mm = pe.matmul(pair_cols(t, t + 1), upto[:], pick[g.par][:, t, :], start=False, stop=False,
                                   skip_group_check=True)
                    if t > 0:
                        last_mm = pe.matmul(pair_cols(0, t), ones_bf[:],
                                       pick[g.par][:, t, :].unsqueeze(1).broadcast_to([P, t, NPAIR]),
                                       start=False, stop=False, skip_group_check=True)
                last_mm.then_inc(counted, 1)

            def graphs(g0, g1, g2, g3, g4, g5):
                if g2:
                    product(g2)
                if g5:
                    count_rest(g5)
                if g0:
                    turn_adj(g0, 0)
                if g4:
                    count_before(g4)
                if g1:
                    turn_xn(g1)
                if g0:
                    turn_adj(g0, 1)
                    turn_adj(g0, 2)
                if g2:
                    neighbour_part(g2)
                if g3:
                    turn_x2(g3)
                    gate(g3)
                if g1:
                    own_part(g1)
                if g0:
                    turn_adj(g0, 3)

            def between(i):
                if i == 1:
                    pe.wait_ge(dve_c, DVE_GATE)
                    pe.wait_ge(pool_c, POOL_ALL)
                    pe.matmul(rank_p, p_row[:], pair_base[:].rearrange("p t q -> p (t q)"), start=True, stop=False,
                              skip_group_check=True)

            pipeline(pe, B, 6, graphs, between=between)
            pe.matmul(pair_cols(0, 1), zero_bf[:], pick[0][:, 0, :], start=False, stop=True,
                      skip_group_check=True).then_inc(count_made, 1)
            pe.wait_ge(tab_ready, 1)
            for c in range(3):
                last_mm = pe.matmul(bank_z[0:1, c * P:(c + 1) * P], tab_cols[:, c:c + 1], ident[:], start=True, stop=True)
            last_mm.then_inc(tab_turned, 1)

            pe.wait_ge(tab_ready, 2)

            def turn_rows(g):
                pe.wait_ge(tn_ready, g.n + 1)
                after(pe, tl_ready, g.n - 1)
                pe.transpose(bank_t[g.par][:, 0:P], tn[g.par][:], ident[:]).then_inc(t_made, 1)

            def first_layer(g):
                pe.wait_ge(tl_ready, g.n + 1)
                pe.wait_ge(w_placed, g.n + 1)
                pe.wait_ge(b_placed, g.n + 1)
                after(pe, hl_ready, g.n - 1)
                for k in range(2):
                    for c in range(HC):
                        o = bank_h[g.par][:, (k * HC + c) * P:(k * HC + c + 1) * P]
                        lead, rest = (w_two[g.slot][:, k, i, c * P:(c + 1) * P] for i in (0, 1))
                        pe.matmul(o, b_two[g.slot][:, k, c * P:(c + 1) * P], ones_bf[:], start=True, stop=False)
                        pe.matmul(o, rest, th[g.par][:], start=False, stop=False)
                        pe.matmul(o, lead, tl[g.par][:], start=False, stop=False)
                        last_mm = pe.matmul(o, lead, th[g.par][:], start=False, stop=True)
                last_mm.then_inc(h_made, 1)

            def second_layer(g):
                pe.wait_ge(hl_ready, g.n + 1)
                after(pe, ya_ready, g.n - 1)
                for k in range(2):
                    o = bank_y[g.par][:, k * D:(k + 1) * D]
                    pe.matmul(o, ones_bf[:], b_two[g.slot][:, k, H:H + D], start=True, stop=False)
                    for c in range(HC):
                        w_lead, w_rest = (w_two[g.slot][:, k, i, c * D:(c + 1) * D] for i in (2, 3))
                        lead, rest = (v[g.par][:, (k * HC + c) * P:(k * HC + c + 1) * P] for v in (hh, hl))
                        pe.matmul(o, rest, w_lead, start=False, stop=False)
                        pe.matmul(o, lead, w_rest, start=False, stop=False)
                        last_mm = pe.matmul(o, lead, w_lead, start=False, stop=(c == HC - 1))
                last_mm.then_inc(y_made, 1)

            def tiles(g0, g1, g2, g3, g4):
                if g4:
                    second_layer(g4)
                if g2:
                    first_layer(g2)
                if g0:
                    turn_rows(g0)

            pipeline(pe, TILES, 5, tiles, unroll=U)


_INS = ["x", "adj", "L0_gnn_gamma", "L0_gnn_beta", "L0_gnn_W_self", "L0_gnn_W_neigh", "L0_ffn_Wg", "L0_ffn_bg",
        "L0_ffn_bias", "L0_ffn_W1", "L0_ffn_b1", "L0_ffn_W2", "L0_ffn_b2"]


def kernel(**inputs):
    import numpy as _np
    import concourse.bacc as _bacc
    from concourse import mybir as _mybir
    from concourse.bass_utils import run_bass_kernel_spmd as _run

    nc = _bacc.Bacc("TRN2", target_bir_lowering=False, num_devices=1)
    arrays, args = {}, []
    for name in _INS:
        a = _np.ascontiguousarray(inputs[name])
        arrays[f"in_{name}_dram"] = a
        args.append(nc.dram_tensor(f"in_{name}_dram", a.shape, _mybir.dt.from_np(a.dtype), kind="ExternalInput").ap())
    shape = inputs["x"].shape
    args.append(nc.dram_tensor("out_dram", shape, _mybir.dt.float32, kind="ExternalOutput").ap())
    gnn_moe_kernel(nc, *args)
    r = _run(nc, [arrays], core_ids=[0])
    return r.results[0]["out_dram"]
```
